# Optimizing a Trainium2 kernel written in Bass

```python
import numpy as np
import jax
import jax.numpy as jnp

def _softmax(x, axis=-1):
    return jax.nn.softmax(x, axis=axis)

def _gelu(x):
    return jax.nn.gelu(x, approximate=True)

def _silu(x):
    return jax.nn.silu(x)

def _sigmoid(x):
    return jax.nn.sigmoid(x)

def _layernorm(x, axis=-1, eps=1e-05):
    m = jnp.mean(x, axis=axis, keepdims=True)
    v = jnp.var(x, axis=axis, keepdims=True)
    return (x - m) / jnp.sqrt(v + eps)

def _scatter_add(tgt, idx, src, axis=0):
    return tgt.at[idx].add(src)

def _segment_sum(src, seg, n):
    return jax.ops.segment_sum(src, seg, n)
kernel_name = 'mk_lm_tower_d1_tok_ids2048_r4_6b1248'

def setup_inputs(seed: int=0):
    np.random.seed(seed)
    _w = jnp.asarray

    def _rec_inputs():
        import jax
        import jax.numpy as jnp
        _rk = jax.random.key(seed)
        x = jax.random.randint(jax.random.fold_in(_rk, 1), (4, 1024), 0, 168, jnp.int32)
        return x
    x = _rec_inputs()

    def _L0_tok_setup():
        import jax, jax.numpy as jnp
        import numpy as np
        NUM_SLOTS = 168
        NUM_CATS = 512
        BATCH, SEQ = (128, 200)
        key = jax.random.key(seed)
        k1, k2 = jax.random.split(key)
        inputs_hour = jax.random.randint(k1, (BATCH, SEQ), 0, NUM_SLOTS)
        catid_time_matrix = jax.random.normal(k2, (NUM_SLOTS, NUM_CATS), dtype=jnp.float32)
        return {'inputs_hour': inputs_hour, 'catid_time_matrix': catid_time_matrix}
    _L0_tok_all = _L0_tok_setup()
    _L0_tok_in = {k: v for k, v in _L0_tok_all.items() if k in ('catid_time_matrix',)}
    del _L0_tok_all

    def _L0_attn_setup():
        import jax, jax.numpy as jnp
        import numpy as np
        import math
        NUM_HEADS = 16
        key = jax.random.key(seed)
        ks = jax.random.split(key, 5)
        B, S, D = (2, 512, 512)
        scale = 1.0 / math.sqrt(D)
        return {'x': jax.random.normal(ks[0], (B, S, D), dtype=jnp.float32), 'Wq': jax.random.normal(ks[1], (D, D), dtype=jnp.float32) * scale, 'Wk': jax.random.normal(ks[2], (D, D), dtype=jnp.float32) * scale, 'Wv': jax.random.normal(ks[3], (D, D), dtype=jnp.float32) * scale, 'Wp': jax.random.normal(ks[4], (D, D), dtype=jnp.float32) * scale}
    _L0_attn_all = _L0_attn_setup()
    _L0_attn_in = {k: v for k, v in _L0_attn_all.items() if k in ('Wq', 'Wk', 'Wv', 'Wp')}
    del _L0_attn_all

    def _L0_ffn_setup():
        import jax, jax.numpy as jnp
        import numpy as np
        B, S, D_IN, D_OUT = (4, 512, 512, 512)
        EPS = 1e-10
        key = jax.random.key(seed)
        kx, kw, kb = jax.random.split(key, 3)
        x = jax.random.normal(kx, (B, S, D_IN), dtype=jnp.float32)
        weight = jax.random.normal(kw, (D_OUT, D_IN), dtype=jnp.float32) * 0.02
        bias = jax.random.normal(kb, (D_OUT,), dtype=jnp.float32) * 0.02
        return {'x': x, 'weight': weight, 'bias': bias}
    _L0_ffn_all = _L0_ffn_setup()
    _L0_ffn_in = {k: v for k, v in _L0_ffn_all.items() if k in ('weight', 'bias')}
    del _L0_ffn_all
    return {'x': x, 'L0_tok_catid_time_matrix': _L0_tok_in['catid_time_matrix'], 'L0_attn_Wq': _L0_attn_in['Wq'], 'L0_attn_Wk': _L0_attn_in['Wk'], 'L0_attn_Wv': _L0_attn_in['Wv'], 'L0_attn_Wp': _L0_attn_in['Wp'], 'L0_ffn_weight': _L0_ffn_in['weight'], 'L0_ffn_bias': _L0_ffn_in['bias']}

def reference(x, L0_tok_catid_time_matrix, L0_attn_Wq, L0_attn_Wk, L0_attn_Wv, L0_attn_Wp, L0_ffn_weight, L0_ffn_bias):
    import jax
    import jax.numpy as jnp

    def _L0_tok_ref(inputs_hour, catid_time_matrix):
        import jax, jax.numpy as jnp
        import numpy as np
        NUM_SLOTS = 168
        NUM_CATS = 512
        BATCH, SEQ = (128, 200)
        probs = jax.nn.softmax(catid_time_matrix, axis=1)
        return probs[inputs_hour]

    def _L0_attn_ref(x, Wq, Wk, Wv, Wp):
        import jax, jax.numpy as jnp
        import numpy as np
        import math
        NUM_HEADS = 16
        B, S, D = x.shape
        H = NUM_HEADS
        hd = D // H
        q = (x @ Wq.T).reshape(B, S, H, hd).transpose(0, 2, 1, 3)
        k = (x @ Wk.T).reshape(B, S, H, hd).transpose(0, 2, 1, 3)
        v = (x @ Wv.T).reshape(B, S, H, hd).transpose(0, 2, 1, 3)
        scores = jnp.einsum('bhqd,bhkd->bhqk', q, k) / jnp.sqrt(jnp.asarray(hd, x.dtype))
        causal = jnp.triu(jnp.ones((S, S), dtype=bool), k=1)
        scores = jnp.where(causal, -jnp.inf, scores)
        attn = jax.nn.softmax(scores, axis=-1)
        out = jnp.einsum('bhqk,bhkd->bhqd', attn, v)
        out = out.transpose(0, 2, 1, 3).reshape(B, S, D)
        return out @ Wp.T

    def _L0_ffn_ref(x, weight, bias):
        import jax, jax.numpy as jnp
        import numpy as np
        B, S, D_IN, D_OUT = (4, 512, 512, 512)
        EPS = 1e-10
        scale = jnp.mean(jnp.abs(weight))
        w_t = jnp.clip(jnp.round(weight / (scale + EPS)), -1.0, 1.0)
        w_ste = weight + jax.lax.stop_gradient(w_t * scale - weight)
        return jnp.einsum('bsi,oi->bso', x, w_ste) + bias
    h = _L0_tok_ref(x, L0_tok_catid_time_matrix)
    h = h + _L0_attn_ref(_layernorm(h, axis=-1), L0_attn_Wq, L0_attn_Wk, L0_attn_Wv, L0_attn_Wp)
    h = h + _L0_ffn_ref(_layernorm(h, axis=-1), L0_ffn_weight, L0_ffn_bias)
    return h

_drawn_inputs = setup_inputs


def setup_inputs(seed=0):
    import zlib

    import numpy as np

    out = dict(_drawn_inputs(seed))
    spreads = {}
    factors = {}
    for name, (base, spread) in spreads.items():
        noise = np.random.default_rng([zlib.crc32(name.encode()), seed]).standard_normal(out[name].shape)
        drawn = base * np.exp(spread * noise) if base else spread * noise
        out[name] = jnp.asarray(drawn.astype(out[name].dtype))
    for name, factor in factors.items():
        out[name] = (out[name] * factor).astype(out[name].dtype)
    return out
```

```python
from contextlib import ExitStack

import concourse.bass as bass
from concourse import mybir

ALU = mybir.AluOpType
ACT = mybir.ActivationFunctionType
AX = mybir.AxisListType
F32 = mybir.dt.float32
F16 = mybir.dt.float16
BF16 = mybir.dt.bfloat16
I32 = mybir.dt.int32
U32 = mybir.dt.uint32
ABSMAX = bass.bass_isa.ReduceOp.absmax
RADD = bass.bass_isa.ReduceOp.add

P = 128
LN_EPS = 1e-5
QUANT_EPS = 1e-10
NEG = -1e30
EXPONENT = 0x7F800000
X_SCALE = 1024.0


def lm_tower_kernel(nc, ids, table, wq_t, wk_t, wv_t, wp_t, wf_t, bias, out, probs_dram):
    B, S = ids.shape
    T, D = table.shape
    H = 16
    HD = D // H
    TB = T - P
    NT = B * S // P
    TPB = S // P
    PAIRS = NT // 2
    KC = D // P
    HG = 3
    NG = -(-H // HG)
    SLOTS = 2 * NG
    GU = H // 2
    heads = [list(range(HG * g, min(HG * g + HG, H))) for g in range(NG)]
    HB0 = HG * (NG // 2)
    V1 = HD + 1
    LT, LA = 2, 3
    O_AT, H_AT, N_AT, XT_AT, Y_AT, OUT_AT = LA + 5, LA + 7, LA + 9, LA + 10, LA + 11, LA + 13
    INV_SQRT = float(HD) ** -0.5

    ctx = ExitStack()
    with ctx:
        def sb(name, shape, dt):
            return ctx.enter_context(nc.sbuf_tensor(name, shape, dt))

        def sem(name):
            return ctx.enter_context(nc.semaphore(name))

        def pb(name):
            return ctx.enter_context(nc.psum_tensor(name, [P, 512], F32))

        tbl = sb("tbl", [P, 2, D], F32)
        wq = sb("wq", [P, KC, D], F32)
        wk = sb("wk", [P, KC, D], F32)
        wv = sb("wv", [P, KC, D], F32)
        wp = sb("wp", [P, KC, D], F32)
        wf = sb("wf", [P, KC, D], F32)
        ids_row = sb("ids_row", [P, B * S], I32)
        ids_col = sb("ids_col", [P, NT], I32)
        bias_b = sb("bias_b", [P, D], F32)
        id_free = sb("id_free", [P, T], F32)
        id_part = sb("id_part", [P, 2], F32)
        ident = sb("ident", [P, P], F32)
        ident16 = sb("ident16", [P, P], BF16)
        tri = sb("tri", [P, P], F16)
        ones16 = sb("ones16", [P, P], F16)
        neg_half = sb("neg_half", [P, 2], F32)
        nmax = sb("nmax", [P, 2], F32)
        esum = sb("esum", [P, 2], F32)
        rsum = sb("rsum", [P, 2], F32)
        probs = sb("probs", [P, 2, D], F32)
        st0 = sb("st0", [P, 2, 6], F32)
        mv0 = sb("mv0", [P, 2, 2], F32)
        var0 = sb("var0", [P, 2], F32)
        rstd0 = sb("rstd0", [P, 2], F32)
        lnt = sb("lnt", [P, 2, D], F32)
        lnt_t = sb("lnt_t", [P, KC, T], F32)
        amax = sb("amax", [P, 4, 2], F32)
        gmax = sb("gmax", [P, 4, 2], F32)
        kmax = sb("kmax", [P, 4], F32)
        kmag = sb("kmag", [P, 4], F32)
        power = sb("power", [P, 4], F32)
        upinv = sb("upinv", [P, 4], F32)
        up = sb("up", [P, 4], F32)
        down = sb("down", [P, 2], F32)
        downs = sb("downs", [P, 2], F32)
        qs = sb("qs", [P, 2, D], F32)
        qstack = sb("qstack", [P, 2, H, 4, HD], F16)
        ks = sb("ks", [P, KC, T], F32)
        khi = sb("khi", [P, KC, T], F16)
        klo = sb("klo", [P, KC, T], F16)
        kstack = sb("kstack", [P, H, T], F16)
        v_a = sb("v_a", [P, H, V1], F32)
        v_b = sb("v_b", [TB, H, V1], F32)
        v_rest = sb("v_rest", [HG * TB, NG, HG * V1], F32)
        wp_s = wq
        packed = ids_row[:].bitcast(F16).rearrange("p (w c n) -> p w c n", w=4, c=KC)
        wp_hi, wp_lo, wneg, wtern = (packed[:, i] for i in range(4))
        wabs = sb("wabs", [P, 1], F32)
        wsum = sb("wsum", [P, 1], F32)
        thr = sb("thr", [P, 4], F32)
        oh_row = sb("oh_row", [P, 2, B * S], F16)
        oh_col = sb("oh_col", [P, B, TPB, T], F16)
        oh_sum = sb("oh_sum", [P, B, TPB, T], F16)
        count = sb("count", [P, NT, T], F32)
        mask = sb("mask", [P, NT, T], BF16)
        NW, NWT = 3, 3
        q4 = sb("q4", [P, H, 2 * P], F16)
        gm = sb("gm", [P, 4, HG], F32)
        count_now = sb("count_now", [P, 2, T], F32)
        W = sb("W", [P, NW, HG, T], F32)
        WC = sb("WC", [P, NW, HG * T], F32)
        WT = sb("WT", [P, NWT, 4, P], F32)
        rden = sb("rden", [P, 2, H], F32)
        o32 = wk[:, 0:2, :]
        parts = oh_sum[:].rearrange("p b c t -> p (b c t)")[:, 0:8 * D].rearrange(
            "p (w s c i) -> p w s c i", w=4, s=2, c=KC)
        o_hi, o_lo, x_hi, x_lo = (parts[:, i] for i in range(4))
        prow = sb("prow", [P, 2, D], F32)
        prow_id = sb("prow_id", [P, 2], I32)
        h2 = wv[:, 2:4, :]
        h2b = tbl
        st = sb("st", [P, 2, 6], F32)
        mv = sb("mv", [P, 2, 2], F32)
        vs = sb("vs", [P, 2], F32)
        rstd = sb("rstd", [P, 2], F32)
        xn = wk[:, 2:4, :]
        y = wv[:, 0:2, :]

        sc = [pb("sc0"), pb("sc1")]
        ring = [pb("ring0"), pb("ring1")]
        av = [pb("av0"), pb("av1")]
        tl = [pb("tl0"), pb("tl1")]

        s_tbl, s_ids_row, s_ids_col, s_bias = sem("tbl_in"), sem("ids_row_in"), sem("ids_col_in"), sem("bias_in")
        s_wq, s_wk, s_wv, s_wp, s_wf = (sem(f"w{n}_in") for n in "qkvpf")
        s_const, s_zero, s_nmax, s_exp0, s_rsum = (sem(n) for n in ("const_set", "zero_set", "nmax_set", "exp0_done", "rsum_set"))
        s_probs, s_pdram, s_st0, s_var0, s_rstd0, s_lnt = (sem(n) for n in ("probs_set", "probs_stored", "st0_set", "var0_set", "rstd0_set", "lnt_set"))
        s_lntt_ps, s_lntt, s_q_ps, s_k_ps, s_v_ps = (sem(n) for n in ("lntT_psum", "lntT_set", "q_psum", "k_psum", "v_psum"))
        s_amax, s_gmax, s_kmax, s_up, s_down = (sem(n) for n in ("amax_set", "gmax_set", "kmax_set", "up_set", "down_set"))
        s_qs, s_qhi, s_qlo, s_qst = (sem(n) for n in ("qs_set", "qhi_set", "qlo_set", "qstack_set"))
        s_ks, s_khi, s_klo, s_kst = (sem(n) for n in ("ks_set", "khi_set", "klo_set", "kstack_in"))
        s_va, s_vb, s_vrest = (sem(n) for n in ("va_set", "vb_set", "vrest_in"))
        s_wps, s_wphi, s_wplo = (sem(n) for n in ("wps_set", "wphi_set", "wplo_set"))
        s_wabs, s_wsum, s_thr, s_wneg, s_wtern = (sem(n) for n in ("wabs_set", "wsum_set", "thr_set", "wneg_set", "wtern_set"))
        s_ohrow, s_ohcol, s_ohsum, s_cnt_ps, s_cnt, s_mask = (sem(n) for n in ("ohrow_set", "ohcol_set", "ohsum_set", "count_psum", "count_set", "mask_set"))
        s_ring_in, s_ring_out = sem("ring_filled"), sem("ring_evacuated")
        s_score, s_gm, s_sub, s_e, s_w = (sem(n) for n in ("scores_ready", "max_ready", "shifted", "exp_ready", "weighted"))
        s_av, s_now = sem("attended"), sem("count_now_set")
        s_rden, s_o, s_ot, s_ohi, s_olo = (sem(n) for n in ("rden_set", "o_ready", "oT_psum", "ohi_ready", "olo_ready"))
        s_h, s_h2, s_st, s_mv, s_vs, s_rstd, s_h2b = (sem(n) for n in ("h_psum", "h2_ready", "stats_ready", "meanvar_ready", "varscaled", "rstd_ready", "h2b_ready"))
        s_xn, s_xt, s_xhi, s_xlo, s_y, s_out = (sem(n) for n in ("xn_ready", "xT_psum", "xhi_ready", "xlo_ready", "y_psum", "out_ready"))
        s_pid, s_prow, s_store = sem("prow_id_set"), [sem("prow_in0"), sem("prow_in1")], [sem("stored0"), sem("stored1")]

        probs_rows = probs_dram
        out_rows = out.rearrange("b (n p) d -> (b n p) d", p=P)
        ids_flat = ids.rearrange("b s -> (b s)")

        def known(p):
            return p.__class__ is int

        def group_behind(p, j, lag):
            back = (j - lag) // SLOTS
            q, jj = p + back, (j - lag) % SLOTS
            if known(p) and not 0 <= q < PAIRS:
                return None
            return q, jj

        def tile_behind(p, j, at):
            if (j - at) % NG:
                return None
            d = (j - at) // NG
            q, s = p + d // 2, d % 2
            if known(p) and not 0 <= q < PAIRS:
                return None
            return q, s

        def gkey(p, j, more=0):
            return p * SLOTS + (j + more)

        def nkey(p, s, more=0):
            return p * 2 + (s + more)

        def wait(eng, s, value):
            if not known(value) or value > 0:
                eng.wait_ge(s, value)

        def units_after(j):
            g = j - NG
            if g < 0:
                return []
            done = min(HG * (g + 1), H) // 2
            return list(range(min(HG * g, H) // 2, done))

        uses = []
        for j in range(SLOTS):
            uses.append(("t", j))
            uses += [("g", u) for u in units_after(j)]
        PER_PAIR = len(uses)

        def ring_index(p, kind, i):
            if known(p) and p < 0:
                return i
            at = uses.index((kind, i))
            if known(p) and p >= PAIRS - 1:
                lost = (GU if p == PAIRS else 0) + sum(k == "g" for k, _ in uses[:at]) * (p == PAIRS - 1)
                return GU - LT + PER_PAIR * p + at - lost
            return p * PER_PAIR + (GU - LT + at)

        def ring_bank(kind, i):
            return (GU - LT + uses.index((kind, i))) % 2

        def ring_of_group(p, j):
            return ring_index(p + (j + LT) // SLOTS, "t", (j + LT) % SLOTS)

        def ring_of_unit(p, u):
            return ring_index(p - 1, "g", u)

        assert PER_PAIR % 2 == 0 and (GU - LT) % 2 == 0

        def bank_at(p, kind, i):
            if known(p):
                return ring[ring_index(p, kind, i) % 2]
            return ring[ring_bank(kind, i)]

        block = ctx.enter_context(nc.Block())

        @block.sync
        def _(sp):
            sp.dma_start(tbl[:, 0, :], table[0:P, :]).then_inc(s_tbl, 16)
            sp.dma_start(tbl[0:TB, 1, :], table[P:T, :]).then_inc(s_tbl, 16)
            sp.dma_start(ids_col[:], ids_flat.rearrange("(n p) -> p n", p=P), allow_slow_non_contiguous=True).then_inc(s_ids_col, 16)
            sp.dma_start(wk[:], wk_t.rearrange("(c p) n -> p c n", p=P)).then_inc(s_wk, 16)
            sp.dma_start(wv[:], wv_t.rearrange("(c p) n -> p c n", p=P)).then_inc(s_wv, 16)
            sp.dma_start(wf[:], wf_t.rearrange("(c p) n -> p c n", p=P)).then_inc(s_wf, 16)
            sp.dma_start(bias_b[:], bias.rearrange("(a d) -> a d", a=1).to_broadcast([P, D])).then_inc(s_bias, 16)
            sp.wait_ge(s_probs, 2)
            sp.dma_start(probs_rows[0:P, :], probs[:, 0, :]).then_inc(s_pdram, 16)
            sp.dma_start(probs_rows[P:T, :], probs[0:TB, 1, :]).then_inc(s_pdram, 16)
            sp.wait_ge(s_khi, 1)
            for r in (0, 1):
                for a in range(4):
                    sp.dma_start(kstack[HD * r:HD * r + HD, a::4, :], khi[HD * a:HD * a + HD, :, :]).then_inc(s_kst, 16)
            sp.wait_ge(s_klo, 1)
            for r in (2, 3):
                for a in range(4):
                    sp.dma_start(kstack[HD * r:HD * r + HD, a::4, :], klo[HD * a:HD * a + HD, :, :]).then_inc(s_kst, 16)
            sp.wait_ge(s_vb, 2)
            sp.wait_ge(s_zero, 2)
            for a in range(HG):
                n = len(range(a, H, HG))
                sp.dma_start(v_rest[TB * a:TB * a + TB, 0:n, V1 * a:V1 * a + V1], v_b[:, a::HG, :]).then_inc(s_vrest, 16)

            def stores(p):
                for j in range(SLOTS):
                    if (t := tile_behind(p, j, OUT_AT)) is not None:
                        q, s = t
                        sp.wait_ge(s_out, nkey(q, s, 1))
                        sp.dma_start(out_rows[bass.ds(q * (2 * P) + s * P, P), :], y[:, s, :]).then_inc(s_store[s], 16)

            stores(0)
            with sp.Fori(1, PAIRS - 1) as p:
                stores(p)
            stores(PAIRS - 1)
            stores(PAIRS)
            for s in range(2):
                sp.wait_ge(s_store[s], 16 * PAIRS)

        @block.gpsimd
        def _(pool):
            nc.gpsimd.iota(id_part[:], [[P, 2]], base=0, channel_multiplier=1,
                           allow_small_or_imprecise_dtypes=True).then_inc(s_const, 1)
            nc.gpsimd.iota(id_free[:], [[1, T]], base=0, channel_multiplier=0,
                           allow_small_or_imprecise_dtypes=True).then_inc(s_const, 1)
            nc.gpsimd.memset(ident[:], 0.0).then_inc(s_const, 1)
            nc.gpsimd.memset(ident16[:], 0.0).then_inc(s_const, 1)
            nc.gpsimd.memset(tri[:], 1.0).then_inc(s_const, 1)
            nc.gpsimd.memset(neg_half[:], -0.5).then_inc(s_const, 1)
            pool.wait_ge(s_const, 6)
            nc.gpsimd.affine_select(out=ident[:], in_=ident[:], compare_op=ALU.not_equal, fill=1.0, base=0,
                                    pattern=[[-1, P]], channel_multiplier=1).then_inc(s_const, 1)
            nc.gpsimd.affine_select(out=ident16[:], in_=ident16[:], compare_op=ALU.not_equal, fill=1.0, base=0,
                                    pattern=[[-1, P]], channel_multiplier=1).then_inc(s_const, 1)
            nc.gpsimd.affine_select(out=tri[:], in_=tri[:], compare_op=ALU.is_ge, fill=0.0, base=0,
                                    pattern=[[1, P]], channel_multiplier=-1).then_inc(s_const, 1)
            nc.gpsimd.memset(ones16[:], 1.0).then_inc(s_const, 1)
            nc.gpsimd.memset(amax[:], 0.0).then_inc(s_zero, 1)
            nc.gpsimd.memset(v_rest[:], 0.0).then_inc(s_zero, 1)
            nc.gpsimd.memset(qstack[:, 1], 0.0).then_inc(s_zero, 1)
            pool.wait_ge(s_var0, 2)
            nc.gpsimd.tensor_tensor(rstd0[:, 0:1], var0[:, 0:1], neg_half[:, 0:1], ALU.pow).then_inc(s_rstd0, 1)
            nc.gpsimd.tensor_tensor(rstd0[0:TB, 1:2], var0[0:TB, 1:2], neg_half[0:TB, 0:1], ALU.pow).then_inc(s_rstd0, 1)
            pool.wait_ge(s_ids_col, 16)

            def fetch_ids(q, s):
                nc.gpsimd.tensor_copy(prow_id[:, s:s + 1], ids_col[:, bass.ds(q * 2 + s, 1)]).then_inc(s_pid, 1)

            def fetch(s):
                nc.gpsimd.indirect_dma_start(
                    prow[:, s, :], None, probs_rows[:, :],
                    bass.IndirectOffsetOnAxis(prow_id[:, s:s + 1].bitcast(U32), 0)).then_inc(s_prow[s], 16)

            for s in range(2):
                fetch_ids(0, s)
            pool.wait_ge(s_pdram, 32)
            pool.wait_ge(s_pid, 2)
            for s in range(2):
                fetch(s)
            pool.wait_ge(s_amax, 7)
            nc.gpsimd.partition_all_reduce(gmax[:].rearrange("p a b -> p (a b)"),
                                           amax[:].rearrange("p a b -> p (a b)"), P, ABSMAX).then_inc(s_gmax, 1)
            pool.wait_ge(s_wabs, 1)
            nc.gpsimd.partition_all_reduce(wsum[:], wabs[:], P, RADD).then_inc(s_wsum, 1)
            pool.wait_ge(s_cnt, NT)
            pool.wait_ge(s_bias, 16)

            def body(p):
                for j in range(SLOTS):
                    if (t := group_behind(p, j, 1)) is not None:
                        q, jj = t
                        s, n = jj // NG, len(heads[jj % NG])
                        if jj % NG == 0:
                            wait(pool, s_w, gkey(q, jj, -NG) * 2)
                            nc.gpsimd.tensor_copy(count_now[:, s:s + 1, :],
                                                  count[:, bass.ds(q * 2 + s, 1), :]).then_inc(s_now, 1)
                            pool.wait_ge(s_now, nkey(q, s, 1))
                        pool.wait_ge(s_e, gkey(q, jj, 1))
                        if not known(q) or gkey(q, jj) >= NW:
                            pool.wait_ge(s_ring_in, ring_of_group(q + (jj - NW) // SLOTS, (jj - NW) % SLOTS) + 1)
                        c = count_now[:, s:s + 1, :]
                        w = W[:, jj % NW, 0:n, :]
                        wide = WC[:, jj % NW, 0:n * P].rearrange("p (a t) -> p a t", a=n)
                        rest = WC[:, jj % NW, HG * P:HG * P + n * TB].rearrange("p (a t) -> p a t", a=n)
                        nc.gpsimd.tensor_tensor(wide, w[:, :, 0:P], c[:, :, 0:P].to_broadcast([P, n, P]), ALU.mult).then_inc(s_w, 1)
                        nc.gpsimd.tensor_tensor(rest, w[:, :, P:T], c[:, :, P:T].to_broadcast([P, n, TB]), ALU.mult).then_inc(s_w, 1)
                    if (t := tile_behind(p, j, N_AT)) is not None:
                        q, s = t
                        more = not known(q) or q < PAIRS - 1
                        if more:
                            pool.wait_ge(s_h2, nkey(q, s, 1))
                            fetch_ids(q + 1, s)
                        pool.wait_ge(s_vs, nkey(q, s, 1))
                        wait(pool, s_xn, nkey(q, s, -1))
                        nc.gpsimd.tensor_tensor(rstd[:, s:s + 1], vs[:, s:s + 1], neg_half[:, 0:1],
                                                ALU.pow).then_inc(s_rstd, 1)
                        wait(pool, s_out, nkey(q, s, -1))
                        if more:
                            pool.wait_ge(s_pid, nkey(q, s, 3))
                        nc.gpsimd.tensor_tensor(h2b[:, s, :], h2[:, s, :], bias_b[:], ALU.add).then_inc(s_h2b, 1)
                        if more:
                            fetch(s)

            body(0)
            body(1)
            with pool.Fori(2, PAIRS - 1) as p:
                body(p)
            body(PAIRS - 1)
            body(PAIRS)

        @block.scalar
        def _(act):
            act.dma_start(ids_row[:], ids_flat.rearrange("(a n) -> a n", a=1).to_broadcast([P, B * S])).then_inc(s_ids_row, 16)
            act.dma_start(wq[:], wq_t.rearrange("(c p) n -> p c n", p=P)).then_inc(s_wq, 16)
            act.dma_start(wp[:], wp_t.rearrange("(c p) n -> p c n", p=P)).then_inc(s_wp, 16)
            for c, n in ((0, P), (1, TB)):
                act.wait_ge(s_nmax, c + 1)
                nc.scalar.activation(probs[0:n, c, :], tbl[0:n, c, :], ACT.Exp, bias=nmax[0:n, c:c + 1],
                                     accum_out=esum[0:n, c:c + 1]).then_inc(s_exp0, 1)
            for half in range(2):
                act.wait_ge(s_lntt_ps, half + 1)
                nc.scalar.copy(lnt_t[:, 2 * half:2 * half + 2, :],
                               tl[half][:, 0:2 * T].rearrange("p (c t) -> p c t", t=T)).then_inc(s_lntt, 1)
            for c in range(TPB):
                for b2 in range(2):
                    e = 2 * c + b2
                    act.wait_ge(s_cnt_ps, e + 1)
                    for b in range(2):
                        nc.scalar.copy(count[:, (2 * b2 + b) * TPB + c, :],
                                       tl[e % 2][:, b * T:b * T + T]).then_inc(s_cnt, 1)
                if c == 0:
                    act.wait_ge(s_zero, 3)
                    for kc, n in ((0, P), (1, TB)):
                        act.wait_ge(s_qs, kc + 1)
                        src = qs[0:n, kc, :].rearrange("p (h d) -> p h d", h=H)
                        nc.scalar.copy(qstack[0:n, kc, :, 0, :], src).then_inc(s_qhi, 1)
                        nc.scalar.copy(qstack[0:n, kc, :, 2, :], src).then_inc(s_qst, 1)
                    act.wait_ge(s_ks, 2)
                    nc.scalar.copy(khi[:], ks[:]).then_inc(s_khi, 1)

            def evacuate_gather(u, bank):
                nc.scalar.copy(q4[:, 2 * u:2 * u + 2, :],
                               bank[:].rearrange("p (h i) -> p h i", h=2)).then_inc(s_ring_out, 1)

            for u in range(GU):
                act.wait_ge(s_ring_in, u + 1)
                evacuate_gather(u, ring[u % 2])
            act.wait_ge(s_wps, 1)
            nc.scalar.copy(wp_hi, wp_s[:]).then_inc(s_wphi, 1)
            act.wait_ge(s_down, 1)

            def body(p):
                for j in range(SLOTS):
                    if (t := group_behind(p, j, LT)) is not None:
                        q, jj = t
                        act.wait_ge(s_ring_in, ring_index(p, "t", j) + 1)
                        wait(act, s_av, gkey(q, jj, 1 - NWT))
                        bank = bank_at(p, "t", j)
                        if len(heads[jj % NG]) == HG:
                            nc.scalar.copy(WT[:, jj % NWT, 0:3, :],
                                           bank[:, 0:3 * P].rearrange("p (a i) -> p a i", a=3))
                            nc.scalar.copy(WT[0:HG * TB, jj % NWT, 3, :], bank[0:HG * TB, 3 * P:4 * P]).then_inc(s_ring_out, 1)
                        else:
                            nc.scalar.copy(WT[:, jj % NWT, 0, :], bank[:, 0:P])
                            nc.scalar.copy(WT[0:TB, jj % NWT, 3, :], bank[0:TB, 3 * P:4 * P]).then_inc(s_ring_out, 1)
                    if not known(p) or p < PAIRS - 1:
                        for u in units_after(j):
                            act.wait_ge(s_ring_in, ring_index(p, "g", u) + 1)
                            evacuate_gather(u, bank_at(p, "g", u))
                    if (t := tile_behind(p, j, O_AT + 1)) is not None:
                        q, s = t
                        act.wait_ge(s_ot, nkey(q, s, 1))
                        wait(act, s_h, nkey(q, s, -1))
                        nc.scalar.copy(o_hi[:, s], tl[s][:].rearrange("p (c i) -> p c i", c=KC)).then_inc(s_ohi, 1)
                    if (t := tile_behind(p, j, XT_AT)) is not None:
                        q, s = t
                        act.wait_ge(s_xt, nkey(q, s, 1))
                        wait(act, s_y, nkey(q, s, -1))
                        nc.scalar.copy(x_hi[:, s], tl[s][:].rearrange("p (c i) -> p c i", c=KC)).then_inc(s_xhi, 1)
                    if (t := group_behind(p, j, 0)) is not None:
                        n = len(heads[j % NG])
                        act.wait_ge(s_sub, gkey(p, j, 1))
                        w = W[:, j % NW, 0:n, :]
                        nc.scalar.activation(w, w, ACT.Exp, scale=down[:, 0:1]).then_inc(s_e, 1)

            body(0)
            body(1)
            with act.Fori(2, PAIRS - 1) as p:
                body(p)
            body(PAIRS - 1)
            body(PAIRS)

        @block.vector
        def _(dve):
            dve.wait_ge(s_tbl, 32)
            for c, n in ((0, P), (1, TB)):
                nc.vector.tensor_reduce(nmax[0:n, c:c + 1], tbl[0:n, c, :], AX.X, ALU.max,
                                        negate=True).then_inc(s_nmax, 1)
            for c, n in ((0, P), (1, TB)):
                dve.wait_ge(s_exp0, c + 1)
                nc.vector.reciprocal(rsum[0:n, c:c + 1], esum[0:n, c:c + 1]).then_inc(s_rsum, 1)
                dve.wait_ge(s_rsum, c + 1)
                nc.vector.tensor_scalar(probs[0:n, c, :], probs[0:n, c, :], rsum[0:n, c:c + 1], None,
                                        ALU.mult).then_inc(s_probs, 1)
            for c, n in ((0, P), (1, TB)):
                dve.wait_ge(s_probs, c + 1)
                nc.vector.bn_stats(st0[0:n, c, :], probs[0:n, c, :]).then_inc(s_st0, 1)
                dve.wait_ge(s_st0, 2 * c + 1)
                nc.vector.bn_aggr(mv0[0:n, c, :], st0[0:n, c, :]).then_inc(s_st0, 1)
                dve.wait_ge(s_st0, 2 * c + 2)
                nc.vector.tensor_scalar(var0[0:n, c:c + 1], mv0[0:n, c, 1:2], LN_EPS, None, ALU.add).then_inc(s_var0, 1)
            dve.wait_ge(s_ids_col, 16)
            dve.wait_ge(s_const, 10)
            nc.vector.tensor_tensor(
                oh_col[:].rearrange("p b c t -> p (b c) t"), ids_col[:].unsqueeze(2).to_broadcast([P, NT, T]),
                id_free[:].unsqueeze(1).to_broadcast([P, NT, T]), ALU.is_equal).then_inc(s_ohcol, 1)
            for c, n in ((0, P), (1, TB)):
                dve.wait_ge(s_rstd0, c + 1)
                nc.vector.tensor_scalar(lnt[0:n, c, :], probs[0:n, c, :], mv0[0:n, c, 0:1], rstd0[0:n, c:c + 1],
                                        ALU.subtract, ALU.mult).then_inc(s_lnt, 1)
            dve.wait_ge(s_ohcol, 1)
            nc.vector.tensor_copy(oh_sum[:, :, 1, :], oh_col[:, :, 0, :]).then_inc(s_ohsum, 1)
            for c in range(2, TPB):
                dve.wait_ge(s_ohsum, c - 1)
                nc.vector.tensor_tensor(oh_sum[:, :, c, :], oh_sum[:, :, c - 1, :], oh_col[:, :, c - 1, :],
                                        ALU.add).then_inc(s_ohsum, 1)
            dve.wait_ge(s_ids_row, 16)
            for c in range(2):
                nc.vector.tensor_scalar(oh_row[:, c, :], ids_row[:], id_part[:, c:c + 1], None,
                                        ALU.is_equal).then_inc(s_ohrow, 1)
            dve.wait_ge(s_zero, 1)
            for c in range(2):
                dve.wait_ge(s_k_ps, c + 1)
                nc.vector.tensor_reduce(amax[:, 1, c:c + 1], av[c][:, 0:2 * T], AX.X, ALU.max,
                                        apply_absolute_value=True).then_inc(s_amax, 1)
            for c, n in ((0, P), (1, TB)):
                dve.wait_ge(s_q_ps, c + 1)
                nc.vector.tensor_reduce(amax[0:n, 0, c:c + 1], sc[c][0:n, :], AX.X, ALU.max,
                                        apply_absolute_value=True).then_inc(s_amax, 1)
            for c, n in ((0, P), (1, TB)):
                dve.wait_ge(s_v_ps, c + 1)
                nc.vector.tensor_reduce(amax[0:n, 2, c:c + 1], ring[c][0:n, :], AX.X, ALU.max,
                                        apply_absolute_value=True).then_inc(s_amax, 1)
            dve.wait_ge(s_wp, 16)
            nc.vector.tensor_reduce(amax[:, 3, 0:1], wp[:].rearrange("p c n -> p (c n)"), AX.X, ALU.max,
                                    apply_absolute_value=True).then_inc(s_amax, 1)
            dve.wait_ge(s_gmax, 1)
            nc.vector.tensor_reduce(kmax[:], gmax[:], AX.X, ALU.max).then_inc(s_kmax, 1)
            dve.wait_ge(s_kmax, 1)
            nc.vector.tensor_scalar(kmag[:], kmax[:], 1e-18, None, ALU.max).then_inc(s_kmax, 1)
            dve.wait_ge(s_kmax, 2)
            nc.vector.tensor_scalar(power[:].bitcast(U32), kmag[:].bitcast(U32), EXPONENT, None,
                                    ALU.bitwise_and).then_inc(s_kmax, 1)
            nc.vector.tensor_scalar(upinv[:].bitcast(U32), kmag[:].bitcast(U32), EXPONENT, EXPONENT,
                                    ALU.bitwise_and, ALU.bitwise_xor).then_inc(s_kmax, 1)
            dve.wait_ge(s_kmax, 4)
            nc.vector.tensor_scalar(up[:], upinv[:], 4096.0, None, ALU.mult).then_inc(s_up, 1)
            nc.vector.tensor_tensor(downs[:], power[:, 0:4:2], power[:, 1:4:2], ALU.mult).then_inc(s_kmax, 1)
            dve.wait_ge(s_kmax, 5)
            nc.vector.tensor_scalar(down[:, 0:1], downs[:, 0:1], 2.0 ** -26, INV_SQRT, ALU.mult, ALU.mult)
            nc.vector.tensor_scalar(down[:, 1:2], downs[:, 1:2], 2.0 ** -26, None, ALU.mult).then_inc(s_down, 1)
            dve.wait_ge(s_up, 1)
            for kc, n in ((0, P), (1, TB)):
                nc.vector.tensor_scalar(qs[0:n, kc, :], sc[kc][0:n, :], up[0:n, 0:1], None, ALU.mult).then_inc(s_qs, 1)
            for c in range(2):
                nc.vector.tensor_scalar(ks[:, 2 * c:2 * c + 2, :].rearrange("p c t -> p (c t)"), av[c][:, 0:2 * T],
                                        up[:, 1:2], None, ALU.mult).then_inc(s_ks, 1)
            for kc, n in ((0, P), (1, TB)):
                dve.wait_ge(s_qs, kc + 1)
                dve.wait_ge(s_qhi, kc + 1)
                nc.vector.tensor_tensor(qstack[0:n, kc, :, 1, :], qs[0:n, kc, :].rearrange("p (h d) -> p h d", h=H),
                                        qstack[0:n, kc, :, 0, :], ALU.subtract).then_inc(s_qlo, 1)
                dve.wait_ge(s_qlo, kc + 1)
                nc.vector.tensor_copy(qstack[0:n, kc, :, 3, :], qstack[0:n, kc, :, 1, :]).then_inc(s_qst, 1)
            dve.wait_ge(s_khi, 1)
            dve.wait_ge(s_ks, 2)
            nc.vector.tensor_tensor(klo[:], ks[:], khi[:], ALU.subtract).then_inc(s_klo, 1)
            nc.vector.tensor_scalar(v_b[:, :, 0:HD], ring[1][0:TB, :].rearrange("p (h d) -> p h d", h=H), up[0:TB, 2:3],
                                    None, ALU.mult).then_inc(s_vb, 1)
            nc.vector.memset(v_b[:, :, HD:V1], 1.0).then_inc(s_vb, 1)
            nc.vector.tensor_scalar(v_a[:, :, 0:HD], ring[0][:].rearrange("p (h d) -> p h d", h=H), up[:, 2:3],
                                    None, ALU.mult).then_inc(s_va, 1)
            nc.vector.memset(v_a[:, :, HD:V1], 1.0).then_inc(s_va, 1)
            dve.wait_ge(s_cnt, NT)
            for half in range(2):
                h = slice(half * NT // 2, (half + 1) * NT // 2)
                nc.vector.tensor_scalar(mask[:, h, :], count[:, h, :], 0.0, NEG, ALU.is_equal, ALU.mult).then_inc(s_mask, 1)
            dve.wait_ge(s_q_ps, 2)
            nc.vector.tensor_scalar(wp_s[:], wp[:], up[:, 3:4], None, ALU.mult).then_inc(s_wps, 1)
            dve.wait_ge(s_wf, 16)
            nc.vector.tensor_reduce(wabs[:], wf[:].rearrange("p c n -> p (c n)"), AX.X, ALU.add,
                                    apply_absolute_value=True).then_inc(s_wabs, 1)
            dve.wait_ge(s_wphi, 1)
            dve.wait_ge(s_wps, 1)
            nc.vector.tensor_tensor(wp_lo, wp_s[:], wp_hi, ALU.subtract).then_inc(s_wplo, 1)
            dve.wait_ge(s_wsum, 1)
            nc.vector.tensor_scalar(thr[:, 0:1], wsum[:], 1.0 / (D * D), None, ALU.mult).then_inc(s_thr, 1)
            dve.wait_ge(s_thr, 1)
            nc.vector.tensor_scalar(thr[:, 1:2], thr[:, 0:1], QUANT_EPS, 0.5, ALU.add, ALU.mult).then_inc(s_thr, 1)
            nc.vector.tensor_scalar(thr[:, 3:4], thr[:, 0:1], 1.0 / X_SCALE, None, ALU.mult).then_inc(s_thr, 1)
            dve.wait_ge(s_thr, 3)
            nc.vector.tensor_scalar(thr[:, 2:3], thr[:, 1:2], -1.0, None, ALU.mult).then_inc(s_thr, 1)
            dve.wait_ge(s_thr, 4)
            nc.vector.tensor_scalar(wneg, wf[:], thr[:, 2:3], None, ALU.is_lt).then_inc(s_wneg, 1)
            dve.wait_ge(s_wneg, 1)
            nc.vector.scalar_tensor_tensor(out=wtern.rearrange("p c n -> p (c n)"),
                                           in0=wf[:].rearrange("p c n -> p (c n)"), scalar=thr[:, 1:2],
                                           in1=wneg.rearrange("p c n -> p (c n)"), op0=ALU.is_gt,
                                           op1=ALU.subtract).then_inc(s_wtern, 1)
            dve.wait_ge(s_down, 1)

            def body(p):
                for j in range(SLOTS):
                    if group_behind(p, j, 0) is not None:
                        n = len(heads[j % NG])
                        dve.wait_ge(s_score, gkey(p, j, 1))
                        bank = sc[j % 2][:, 0:n * T].rearrange("p (a t) -> p a t", a=n)
                        nc.vector.tensor_reduce(gm[:, j % 4, 0:n], bank, AX.X, ALU.max).then_inc(s_gm, 1)
                        dve.wait_ge(s_gm, gkey(p, j, 1))
                        wait(dve, s_w, gkey(p, j, 1 - NW) * 2)
                        nc.vector.tensor_tensor(W[:, j % NW, 0:n, :], bank,
                                                gm[:, j % 4, 0:n].unsqueeze(2).to_broadcast([P, n, T]),
                                                ALU.subtract).then_inc(s_sub, 1)
                    if (t := tile_behind(p, j, O_AT)) is not None:
                        q, s = t
                        dve.wait_ge(s_av, gkey(q, NG * s + NG - 1, 1))
                        for b, (h0, h1) in enumerate(((0, HB0), (HB0, H))):
                            a = av[b][:, 0:(h1 - h0) * V1].rearrange("p (h d) -> p h d", d=V1)
                            nc.vector.reciprocal(rden[:, s, h0:h1].unsqueeze(2), a[:, :, HD:V1]).then_inc(s_rden, 1)
                        wait(dve, s_ot, nkey(q, s, -1))
                        for b, (h0, h1) in enumerate(((0, HB0), (HB0, H))):
                            a = av[b][:, 0:(h1 - h0) * V1].rearrange("p (h d) -> p h d", d=V1)
                            dve.wait_ge(s_rden, nkey(q, s) * 2 + (b + 1))
                            nc.vector.tensor_tensor(
                                o32[:, s, HD * h0:HD * h1].rearrange("p (h d) -> p h d", d=HD), a[:, :, 0:HD],
                                rden[:, s, h0:h1].unsqueeze(2).to_broadcast([P, h1 - h0, HD]), ALU.mult).then_inc(s_o, 1)
                    if (t := tile_behind(p, j, O_AT + 1)) is not None:
                        q, s = t
                        dve.wait_ge(s_ohi, nkey(q, s, 1))
                        wait(dve, s_h, nkey(q, s, -1))
                        nc.vector.tensor_tensor(o_lo[:, s], tl[s][:].rearrange("p (c i) -> p c i", c=KC), o_hi[:, s],
                                                ALU.subtract).then_inc(s_olo, 1)
                    if (t := tile_behind(p, j, N_AT)) is not None:
                        q, s = t
                        dve.wait_ge(s_h, nkey(q, s, 1))
                        dve.wait_ge(s_prow[s], q * 16 + 16)
                        wait(dve, s_h2b, nkey(q, s, -1))
                        nc.vector.scalar_tensor_tensor(out=h2[:, s, :], in0=tl[s][:], scalar=down[:, 1:2],
                                                       in1=prow[:, s, :], op0=ALU.mult, op1=ALU.add).then_inc(s_h2, 1)
                        dve.wait_ge(s_h2, nkey(q, s, 1))
                        nc.vector.bn_stats(st[:, s, :], h2[:, s, :]).then_inc(s_st, 1)
                        dve.wait_ge(s_down, 1)
                        dve.wait_ge(s_st, nkey(q, s, 1))
                        nc.vector.bn_aggr(mv[:, s, :], st[:, s, :]).then_inc(s_mv, 1)
                        dve.wait_ge(s_mv, nkey(q, s, 1))
                        wait(dve, s_rstd, nkey(q, s, -1))
                        nc.vector.tensor_scalar(vs[:, s:s + 1], mv[:, s, 1:2], LN_EPS, X_SCALE ** -2, ALU.add,
                                                ALU.mult).then_inc(s_vs, 1)
                    if (t := tile_behind(p, j, XT_AT)) is not None:
                        q, s = t
                        dve.wait_ge(s_rstd, nkey(q, s, 1))
                        wait(dve, s_xt, nkey(q, s, -1))
                        nc.vector.tensor_scalar(xn[:, s, :], h2[:, s, :], mv[:, s, 0:1], rstd[:, s:s + 1],
                                                ALU.subtract, ALU.mult).then_inc(s_xn, 1)
                    if (t := tile_behind(p, j, Y_AT)) is not None:
                        q, s = t
                        dve.wait_ge(s_xhi, nkey(q, s, 1))
                        wait(dve, s_y, nkey(q, s, -1))
                        nc.vector.tensor_tensor(x_lo[:, s], tl[s][:].rearrange("p (c i) -> p c i", c=KC), x_hi[:, s],
                                                ALU.subtract).then_inc(s_xlo, 1)
                    if (t := tile_behind(p, j, OUT_AT)) is not None:
                        q, s = t
                        dve.wait_ge(s_y, nkey(q, s, 1))
                        dve.wait_ge(s_h2b, nkey(q, s, 1))
                        wait(dve, s_store[s], q * 16)
                        nc.vector.scalar_tensor_tensor(out=y[:, s, :], in0=tl[s][:], scalar=thr[:, 3:4],
                                                       in1=h2b[:, s, :], op0=ALU.mult, op1=ALU.add).then_inc(s_out, 1)

            body(0)
            body(1)
            with dve.Fori(2, PAIRS - 1) as p:
                body(p)
            body(PAIRS - 1)
            body(PAIRS)

        @block.tensor
        def _(pe):
            pe.wait_ge(s_const, 10)
            pe.wait_ge(s_lnt, 2)
            for half in range(2):
                for c in range(2):
                    cc = 2 * half + c
                    nc.tensor.transpose(tl[half][:, c * T:c * T + P], lnt[:, 0, cc * P:cc * P + P], ident[:])
                    mm = nc.tensor.transpose(tl[half][:, c * T + P:c * T + T], lnt[0:TB, 1, cc * P:cc * P + P],
                                             ident[0:TB, 0:TB])
                mm.then_inc(s_lntt_ps, 1)
            pe.wait_ge(s_lntt, 2)
            pe.wait_ge(s_wk, 16)
            for g in range(KC):
                for c in range(KC):
                    mm = nc.tensor.matmul(av[g // 2][:, (g % 2) * T:(g % 2) * T + T], wk[:, c, g * P:g * P + P],
                                          lnt_t[:, c, :], start=(c == 0), stop=(c == KC - 1), skip_group_check=True)
                if g % 2:
                    mm.then_inc(s_k_ps, 1)
            for w, loaded, banks, made in ((wq, s_wq, sc, s_q_ps), (wv, s_wv, ring, s_v_ps)):
                pe.wait_ge(loaded, 16)
                for kc, (t0, n) in enumerate(((0, P), (P, TB))):
                    for c in range(KC):
                        mm = nc.tensor.matmul(banks[kc][0:n, :], lnt_t[:, c, t0:t0 + n], w[:, c, :],
                                              start=(c == 0), stop=(c == KC - 1))
                    mm.then_inc(made, 1)
            pe.wait_ge(s_ohcol, 1)
            for c in range(TPB):
                if c:
                    pe.wait_ge(s_ohsum, c)
                for b2 in range(2):
                    e = 2 * c + b2
                    wait(pe, s_cnt, 2 * (e - 1))
                    bank = tl[e % 2][:, 0:2 * T].rearrange("p (b t) -> p b t", b=2)
                    mm = nc.tensor.matmul(bank, tri[:], oh_col[:, 2 * b2:2 * b2 + 2, c, :], start=True, stop=(c == 0))
                    if c:
                        mm = nc.tensor.matmul(bank, ones16[:], oh_sum[:, 2 * b2:2 * b2 + 2, c, :],
                                              start=False, stop=True)
                    mm.then_inc(s_cnt_ps, 1)

            def gather(pair, u, bank):
                for a in range(2):
                    for kc in range(2):
                        rhs = oh_row[:, kc, bass.ds(pair * (2 * P), 2 * P)]
                        mm = nc.tensor.matmul(bank[:, a * 2 * P:(a + 1) * 2 * P],
                                              qstack[:, kc, 2 * u + a, :, :].rearrange("p r d -> p (r d)"), rhs,
                                              start=(kc == 0), stop=(kc == 1))
                mm.then_inc(s_ring_in, 1)

            pe.wait_ge(s_ohrow, 2)
            pe.wait_ge(s_qst, 4)
            pe.wait_ge(s_qhi, 2)
            pe.wait_ge(s_zero, 3)
            pe.wait_ge(s_va, 2)
            for u in range(GU):
                wait(pe, s_ring_out, u - 1)
                gather(0, u, ring[u % 2])
            pe.wait_ge(s_ks, 2)
            pe.wait_ge(s_mask, 2)
            pe.wait_ge(s_kst, 16 * 16)
            pe.wait_ge(s_vrest, 16 * HG)

            def scores(p, j):
                s, g = j // NG, j % NG
                n = len(heads[g])
                pe.wait_ge(s_ring_out, ring_of_unit(p, heads[g][-1] // 2) + 1)
                wait(pe, s_sub, gkey(p, j, -1))
                m = mask[:, bass.ds(p * 2 + s, 1), :].to_broadcast([P, n, T])
                nc.tensor.matmul(sc[j % 2][:, 0:n * T], ident16[:], m, start=True, stop=False, skip_group_check=True)
                for a, h in enumerate(heads[g]):
                    mm = nc.tensor.matmul(sc[j % 2][:, a * T:a * T + T], q4[:, h, s * P:s * P + P], kstack[:, h, :],
                                          start=False, stop=(a == n - 1), skip_group_check=True)
                mm.then_inc(s_score, 1)

            def transposes(p, j):
                q, jj = group_behind(p, j, LT)
                n = len(heads[jj % NG])
                e = ring_index(p, "t", j)
                pe.wait_ge(s_ring_out, e - 1)
                pe.wait_ge(s_w, gkey(q, jj, 1) * 2)
                bank, w = bank_at(p, "t", j), WC[:, jj % NW, :]
                for a in range(n):
                    nc.tensor.transpose(bank[:, a * P:a * P + P], w[:, a * P:a * P + P], ident[:])
                nc.tensor.transpose(bank[0:n * TB, 3 * P:4 * P], w[:, HG * P:HG * P + n * TB], ident[:]).then_inc(s_ring_in, 1)

            def attend(q, jj):
                s, g = jj // NG, jj % NG
                n = len(heads[g])
                pe.wait_ge(s_ring_out, ring_of_group(q, jj) + 1)
                if g == 0:
                    wait(pe, s_o, nkey(q, s) * 2)
                b = 0 if heads[g][0] < HB0 else 1
                first = heads[g][0] in (0, HB0)
                for a, h in enumerate(heads[g]):
                    at = V1 * (h - HB0 * b)
                    nc.tensor.matmul(av[b][:, at:at + V1], WT[:, jj % NWT, a, :], v_a[:, h, :],
                                     start=(first and a == 0), stop=False, skip_group_check=True)
                at = V1 * (heads[g][0] - HB0 * b)
                nc.tensor.matmul(av[b][:, at:at + n * V1], WT[0:n * TB, jj % NWT, 3, :], v_rest[0:n * TB, g, 0:n * V1],
                                 start=False, stop=(g in (NG // 2 - 1, NG - 1)), skip_group_check=True).then_inc(s_av, 1)

            def turn(src, s):
                for c in range(KC):
                    mm = nc.tensor.transpose(tl[s][:, c * P:c * P + P], src[:, s, c * P:c * P + P], ident[:])
                return mm

            def project(s, cs):
                for c in cs:
                    nc.tensor.matmul(tl[s][:], o_hi[:, s, c, :], wp_hi[:, c, :], start=(c == 0), stop=False)
                    nc.tensor.matmul(tl[s][:], o_hi[:, s, c, :], wp_lo[:, c, :], start=False, stop=False)
                    mm = nc.tensor.matmul(tl[s][:], o_lo[:, s, c, :], wp_hi[:, c, :], start=False, stop=(c == KC - 1))
                return mm

            def body(p):
                for j in range(SLOTS):
                    if group_behind(p, j, 0) is not None:
                        scores(p, j)
                    if group_behind(p, j, LT) is not None:
                        transposes(p, j)
                    if not known(p) or p < PAIRS - 1:
                        for u in units_after(j):
                            pe.wait_ge(s_ring_out, ring_index(p, "g", u) - 1)
                            gather(p + 1, u, bank_at(p, "g", u))
                    if (t := group_behind(p, j, LA)) is not None:
                        attend(*t)
                    if (t := tile_behind(p, j, O_AT + 1)) is not None:
                        q, s = t
                        pe.wait_ge(s_o, nkey(q, s) * 2 + 2)
                        wait(pe, s_out, nkey(q, s, -1))
                        turn(o32, s).then_inc(s_ot, 1)
                    if (t := tile_behind(p, j, H_AT)) is not None:
                        q, s = t
                        pe.wait_ge(s_olo, nkey(q, s, 1))
                        if known(p) and p == 0:
                            pe.wait_ge(s_wplo, 1)
                        project(s, (0, 1))
                    if (t := tile_behind(p, j, H_AT + 1)) is not None:
                        q, s = t
                        project(s, (2, 3)).then_inc(s_h, 1)
                    if (t := tile_behind(p, j, XT_AT)) is not None:
                        q, s = t
                        pe.wait_ge(s_xn, nkey(q, s, 1))
                        turn(xn, s).then_inc(s_xt, 1)
                    if (t := tile_behind(p, j, Y_AT + 1)) is not None:
                        q, s = t
                        pe.wait_ge(s_xlo, nkey(q, s, 1))
                        if known(p) and p <= 1:
                            pe.wait_ge(s_wtern, 1)
                        for c in range(KC):
                            nc.tensor.matmul(tl[s][:], x_hi[:, s, c, :], wtern[:, c, :], start=(c == 0), stop=False)
                            mm = nc.tensor.matmul(tl[s][:], x_lo[:, s, c, :], wtern[:, c, :], start=False,
                                                  stop=(c == KC - 1))
                        mm.then_inc(s_y, 1)

            body(0)
            body(1)
            with pe.Fori(2, PAIRS - 1) as p:
                body(p)
            body(PAIRS - 1)
            body(PAIRS)


def kernel(x, L0_tok_catid_time_matrix, L0_attn_Wq, L0_attn_Wk, L0_attn_Wv, L0_attn_Wp, L0_ffn_weight, L0_ffn_bias):
    import numpy as np
    import concourse.bacc as bacc
    from concourse.bass_utils import run_bass_kernel_spmd

    nc = bacc.Bacc("TRN2", target_bir_lowering=False, num_devices=1)
    arrays = {
        "ids": np.ascontiguousarray(x),
        "table": np.ascontiguousarray(L0_tok_catid_time_matrix),
        "wq_t": np.ascontiguousarray(np.asarray(L0_attn_Wq).T),
        "wk_t": np.ascontiguousarray(np.asarray(L0_attn_Wk).T),
        "wv_t": np.ascontiguousarray(np.asarray(L0_attn_Wv).T),
        "wp_t": np.ascontiguousarray(np.asarray(L0_attn_Wp).T),
        "wf_t": np.ascontiguousarray(np.asarray(L0_ffn_weight).T),
        "bias": np.ascontiguousarray(L0_ffn_bias),
    }
    args = [nc.dram_tensor(n, a.shape, mybir.dt.from_np(a.dtype), kind="ExternalInput").ap() for n, a in arrays.items()]
    shape = (*arrays["ids"].shape, arrays["table"].shape[1])
    out = nc.dram_tensor("out", shape, F32, kind="ExternalOutput").ap()
    scratch = nc.dram_tensor("probs_by_id", arrays["table"].shape, F32, kind="Internal").ap()
    lm_tower_kernel(nc, *args, out, scratch)
    result = run_bass_kernel_spmd(nc, [arrays], core_ids=[0])
    return result.results[0]["out"]
```

```python
from contextlib import ExitStack

import concourse.bass as bass
from concourse import mybir

ALU = mybir.AluOpType
ACT = mybir.ActivationFunctionType
AX = mybir.AxisListType
F32 = mybir.dt.float32
F16 = mybir.dt.float16
BF16 = mybir.dt.bfloat16
I32 = mybir.dt.int32
U32 = mybir.dt.uint32
ABSMAX = bass.bass_isa.ReduceOp.absmax
RADD = bass.bass_isa.ReduceOp.add

P = 128
LN_EPS = 1e-5
QUANT_EPS = 1e-10
NEG = -1e30
EXPONENT = 0x7F800000
X_SCALE = 1024.0


def lm_tower_kernel(nc, ids, table, wq_t, wk_t, wv_t, wp_t, wf_t, bias, out, probs_dram):
    B, S = ids.shape
    T, D = table.shape
    H = 16
    HD = D // H
    TB = T - P
    NT = B * S // P
    TPB = S // P
    PAIRS = NT // 2
    KC = D // P
    HG = 3
    NG = -(-H // HG)
    SLOTS = 2 * NG
    UH = 4
    GU = H // UH
    heads = [list(range(HG * g, min(HG * g + HG, H))) for g in range(NG)]
    HB0 = HG * (NG // 2)
    V1 = HD + 1
    LW, LT, LA = 1, 3, 4
    O_AT = (LA + NG // 2, LA + NG)
    OT_AT = O_AT[1] + 1
    OL_AT = OT_AT + 1
    H_AT = {OL_AT: range(0, 4), OL_AT + 1: range(4, 8), OL_AT + 2: range(8, 12)}
    N_AT = OL_AT + 3
    XN_AT = N_AT + 1
    XT_AT = XN_AT + 1
    XL_AT = XT_AT + 2
    Y_AT = {XL_AT + 1: range(0, 3), XL_AT + 2: range(3, 8)}
    B_AT = XL_AT + 1
    OUT_AT = XL_AT + 3
    BY_DVE = (1,)
    PEELED = 3
    INV_SQRT = float(HD) ** -0.5

    ctx = ExitStack()
    with ctx:
        def sb(name, shape, dt):
            return ctx.enter_context(nc.sbuf_tensor(name, shape, dt))

        def sem(name):
            return ctx.enter_context(nc.semaphore(name))

        def pb(name):
            return ctx.enter_context(nc.psum_tensor(name, [P, 512], F32))

        tbl = sb("tbl", [P, 2, D], F32)
        wq = sb("wq", [P, KC, D], F32)
        wk = sb("wk", [P, KC, D], F32)
        wv = sb("wv", [P, KC, D], F32)
        wp = sb("wp", [P, KC, D], F32)
        wf = sb("wf", [P, KC, D], F32)
        ids_row = sb("ids_row", [P, B * S], I32)
        ids_col = sb("ids_col", [P, NT], I32)
        bias_b = sb("bias_b", [P, D], F32)
        id_free = sb("id_free", [P, T], F32)
        id_part = sb("id_part", [P, 2], F32)
        ident = sb("ident", [P, P], F32)
        ident16 = sb("ident16", [P, P], BF16)
        tri = sb("tri", [P, P], F16)
        ones16 = sb("ones16", [P, P], F16)
        neg_half = sb("neg_half", [P, 2], F32)
        nmax = sb("nmax", [P, 2], F32)
        esum = sb("esum", [P, 2], F32)
        rsum = sb("rsum", [P, 2], F32)
        probs = sb("probs", [P, 2, D], F32)
        st0 = sb("st0", [P, 2, 6], F32)
        mv0 = sb("mv0", [P, 2, 2], F32)
        var0 = sb("var0", [P, 2], F32)
        rstd0 = sb("rstd0", [P, 2], F32)
        lnt = sb("lnt", [P, 2, D], F32)
        lnt_t = sb("lnt_t", [P, KC, T], F32)
        amax = sb("amax", [P, 4, 2], F32)
        gmax = sb("gmax", [P, 4, 2], F32)
        kmax = sb("kmax", [P, 4], F32)
        kmag = sb("kmag", [P, 4], F32)
        power = sb("power", [P, 4], F32)
        upinv = sb("upinv", [P, 4], F32)
        up = sb("up", [P, 4], F32)
        down = sb("down", [P, 2], F32)
        downs = sb("downs", [P, 2], F32)
        qs = sb("qs", [P, 2, D], F32)
        qstack = sb("qstack", [P, 2, H, 2, HD], F16)
        ks = sb("ks", [P, KC, T], F32)
        khi = sb("khi", [P, KC, T], F16)
        klo = sb("klo", [P, KC, T], F16)
        kstack = sb("kstack", [P, H, T], F16)
        v_a = sb("v_a", [P, H, V1], F32)
        v_b = sb("v_b", [TB, H, V1], F32)
        v_rest = sb("v_rest", [HG * TB, NG, HG * V1], F32)
        wp_s = wq
        packed = ids_row[:].bitcast(F16).rearrange("p (w c n) -> p w c n", w=4, c=KC)
        wp_hi, wp_lo, wneg, wtern = (packed[:, i] for i in range(4))
        wabs = sb("wabs", [P, 1], F32)
        wsum = sb("wsum", [P, 1], F32)
        thr = sb("thr", [P, 4], F32)
        oh_row = sb("oh_row", [P, 2, B * S], F16)
        oh_col = sb("oh_col", [P, B, TPB, T], F16)
        oh_sum = sb("oh_sum", [P, B, TPB, T], F16)
        count = sb("count", [P, NT, T], F32)
        mask = sb("mask", [P, NT, T], BF16)
        NW, NWT = 3, 3
        qx = sb("qx", [P, GU, 2, 2 * P], F16)
        q4 = sb("q4", [P, H, 2 * P], F16)
        gm = sb("gm", [P, 4, HG], F32)
        nb = sb("nb", [P, 4, HG], F32)
        count_now = sb("count_now", [P, 2, T], F32)
        W = sb("W", [P, NW, HG, T], F32)
        WC = sb("WC", [P, NW, HG * T], F32)
        WT = sb("WT", [P, NWT, 4, P], F32)
        rden = sb("rden", [P, 2, H], F32)
        o32 = wk[:, 0:2, :]
        parts = oh_sum[:].rearrange("p b c t -> p (b c t)")[:, 0:8 * D].rearrange(
            "p (w s c i) -> p w s c i", w=4, s=2, c=KC)
        o_hi, o_lo, x_hi, x_lo = (parts[:, i] for i in range(4))
        prow = sb("prow", [P, 2, D], F32)
        prow_id = sb("prow_id", [P, 2], I32)
        h2 = wv[:, 2:4, :]
        h2b = tbl
        st = sb("st", [P, 2, 6], F32)
        mv = sb("mv", [P, 2, 2], F32)
        vs = sb("vs", [P, 2], F32)
        rstd = sb("rstd", [P, 2], F32)
        xn = wk[:, 2:4, :]
        y = wv[:, 0:2, :]

        sc = [pb("sc0"), pb("sc1")]
        ring = [pb("ring0"), pb("ring1")]
        av = [pb("av0"), pb("av1")]
        tl = [pb("tl0"), pb("tl1")]

        s_tbl, s_ids_row, s_ids_col, s_bias = sem("tbl_in"), sem("ids_row_in"), sem("ids_col_in"), sem("bias_in")
        s_wq, s_wk, s_wv, s_wp, s_wf = (sem(f"w{n}_in") for n in "qkvpf")
        s_const, s_zero, s_nmax, s_exp0, s_rsum = (sem(n) for n in ("const_set", "zero_set", "nmax_set", "exp0_done", "rsum_set"))
        s_probs, s_pdram, s_st0, s_var0, s_rstd0, s_lnt = (sem(n) for n in ("probs_set", "probs_stored", "st0_set", "var0_set", "rstd0_set", "lnt_set"))
        s_lntt_ps, s_lntt, s_q_ps, s_k_ps, s_v_ps = (sem(n) for n in ("lntT_psum", "lntT_set", "q_psum", "k_psum", "v_psum"))
        s_amax, s_gmax, s_kmax, s_up, s_down = (sem(n) for n in ("amax_set", "gmax_set", "kmax_set", "up_set", "down_set"))
        s_qs, s_qhi, s_qlo = (sem(n) for n in ("qs_set", "qhi_set", "qlo_set"))
        s_ks, s_khi, s_klo, s_kst = (sem(n) for n in ("ks_set", "khi_set", "klo_set", "kstack_in"))
        s_va, s_vb, s_vrest = (sem(n) for n in ("va_set", "vb_set", "vrest_in"))
        s_wps, s_wphi, s_wplo = (sem(n) for n in ("wps_set", "wphi_set", "wplo_set"))
        s_wabs, s_wsum, s_thr, s_wneg, s_wtern = (sem(n) for n in ("wabs_set", "wsum_set", "thr_set", "wneg_set", "wtern_set"))
        s_ohrow, s_ohcol, s_ohsum, s_cnt_ps, s_cnt, s_mask = (sem(n) for n in ("ohrow_set", "ohcol_set", "ohsum_set", "count_psum", "count_set", "mask_set"))
        s_ring_in, s_ring_out = sem("ring_filled"), sem("ring_evacuated")
        s_score, s_gm, s_nb, s_e = (sem(n) for n in ("scores_ready", "max_ready", "shift_ready", "exp_ready"))
        s_wpool, s_wdve = sem("weighted_by_pool"), sem("weighted_by_dve")
        s_q4 = [sem(f"q4_in{u}") for u in range(GU)]
        s_av, s_now = sem("attended"), sem("count_now_set")
        s_rden, s_o, s_ot, s_ohi, s_olo = (sem(n) for n in ("rden_set", "o_ready", "oT_psum", "ohi_ready", "olo_ready"))
        s_h, s_h2, s_st, s_mv, s_vs, s_rstd, s_h2b = (sem(n) for n in ("h_psum", "h2_ready", "stats_ready", "meanvar_ready", "varscaled", "rstd_ready", "h2b_ready"))
        s_xn, s_xt, s_xhi, s_xlo, s_y, s_out = (sem(n) for n in ("xn_ready", "xT_psum", "xhi_ready", "xlo_ready", "y_psum", "out_ready"))
        s_pid, s_prow, s_store = sem("prow_id_set"), [sem("prow_in0"), sem("prow_in1")], [sem("stored0"), sem("stored1")]

        probs_rows = probs_dram
        out_rows = out.rearrange("b (n p) d -> (b n p) d", p=P)
        ids_flat = ids.rearrange("b s -> (b s)")

        def known(p):
            return p.__class__ is int

        def group_behind(p, j, lag):
            back = (j - lag) // SLOTS
            q, jj = p + back, (j - lag) % SLOTS
            if known(p) and not 0 <= q < PAIRS:
                return None
            return q, jj

        def tile_behind(p, j, at):
            if (j - at) % NG:
                return None
            d = (j - at) // NG
            q, s = p + d // 2, d % 2
            if known(p) and not 0 <= q < PAIRS:
                return None
            return q, s

        def gkey(p, j, more=0):
            return p * SLOTS + (j + more)

        def nkey(p, s, more=0):
            return p * 2 + (s + more)

        def wait(eng, s, value):
            if not known(value) or value > 0:
                eng.wait_ge(s, value)

        def units_after(j):
            return [u for u in range(GU) if (UH * u + UH - 1) // HG == j - NG]

        def by_dve(jj):
            return jj % NG in BY_DVE

        DVE_SLOTS = [jj for jj in range(SLOTS) if by_dve(jj)]
        POOL_SLOTS = [jj for jj in range(SLOTS) if not by_dve(jj)]

        def wait_weighted(eng, q, jj):
            if by_dve(jj):
                eng.wait_ge(s_wdve, (q * len(DVE_SLOTS) + (DVE_SLOTS.index(jj) + 1)) * 2)
            else:
                eng.wait_ge(s_wpool, (q * len(POOL_SLOTS) + (POOL_SLOTS.index(jj) + 1)) * 2)

        uses = []
        for j in range(SLOTS):
            uses.append(("t", j))
            uses += [("g", u) for u in units_after(j)]
        PER_PAIR = len(uses)

        def ring_index(p, kind, i):
            if known(p) and p < 0:
                return i
            at = uses.index((kind, i))
            if known(p) and p >= PAIRS - 1:
                lost = (GU if p == PAIRS else 0) + sum(k == "g" for k, _ in uses[:at]) * (p == PAIRS - 1)
                return GU - LT + PER_PAIR * p + at - lost
            return p * PER_PAIR + (GU - LT + at)

        def ring_bank(kind, i):
            return (GU - LT + uses.index((kind, i))) % 2

        def ring_of_group(p, j):
            return ring_index(p + (j + LT) // SLOTS, "t", (j + LT) % SLOTS)

        assert PER_PAIR % 2 == 0

        def bank_at(p, kind, i):
            if known(p):
                return ring[ring_index(p, kind, i) % 2]
            return ring[ring_bank(kind, i)]

        def weight(eng, ops, q, jj, c, done):
            n = len(heads[jj % NG])
            eng.wait_ge(s_e, gkey(q, jj, 1))
            if not known(q) or gkey(q, jj) >= NW:
                eng.wait_ge(s_ring_in, ring_of_group(q + (jj - NW) // SLOTS, (jj - NW) % SLOTS) + 1)
            w = W[:, jj % NW, 0:n, :]
            wide = WC[:, jj % NW, 0:n * P].rearrange("p (a t) -> p a t", a=n)
            rest = WC[:, jj % NW, n * P:n * T].rearrange("p (a t) -> p a t", a=n)
            ops.tensor_tensor(wide, w[:, :, 0:P], c[:, :, 0:P].to_broadcast([P, n, P]), ALU.mult).then_inc(done, 1)
            ops.tensor_tensor(rest, w[:, :, P:T], c[:, :, P:T].to_broadcast([P, n, TB]), ALU.mult).then_inc(done, 1)

        block = ctx.enter_context(nc.Block())

        @block.sync
        def _(sp):
            sp.dma_start(tbl[:, 0, :], table[0:P, :]).then_inc(s_tbl, 16)
            sp.dma_start(tbl[0:TB, 1, :], table[P:T, :]).then_inc(s_tbl, 16)
            sp.dma_start(ids_col[:], ids_flat.rearrange("(n p) -> p n", p=P), allow_slow_non_contiguous=True).then_inc(s_ids_col, 16)
            sp.dma_start(wk[:], wk_t.rearrange("(c p) n -> p c n", p=P)).then_inc(s_wk, 16)
            sp.dma_start(wv[:], wv_t.rearrange("(c p) n -> p c n", p=P)).then_inc(s_wv, 16)
            sp.dma_start(wf[:], wf_t.rearrange("(c p) n -> p c n", p=P)).then_inc(s_wf, 16)
            sp.dma_start(bias_b[:], bias.rearrange("(a d) -> a d", a=1).to_broadcast([P, D])).then_inc(s_bias, 16)
            sp.wait_ge(s_probs, 2)
            sp.dma_start(probs_rows[0:P, :], probs[:, 0, :]).then_inc(s_pdram, 16)
            sp.dma_start(probs_rows[P:T, :], probs[0:TB, 1, :]).then_inc(s_pdram, 16)
            sp.wait_ge(s_khi, 1)
            for r in (0, 1):
                for a in range(4):
                    sp.dma_start(kstack[HD * r:HD * r + HD, a::4, :], khi[HD * a:HD * a + HD, :, :]).then_inc(s_kst, 16)
            sp.wait_ge(s_klo, 1)
            for r in (2, 3):
                for a in range(4):
                    sp.dma_start(kstack[HD * r:HD * r + HD, a::4, :], klo[HD * a:HD * a + HD, :, :]).then_inc(s_kst, 16)
            sp.wait_ge(s_vb, 2)
            sp.wait_ge(s_zero, 2)
            for a in range(HG):
                n = len(range(a, H, HG))
                sp.dma_start(v_rest[TB * a:TB * a + TB, 0:n, V1 * a:V1 * a + V1], v_b[:, a::HG, :]).then_inc(s_vrest, 16)

            def spread(p, u):
                for odd in range(2):
                    for half in range(2):
                        sp.dma_start(q4[64 * half:64 * half + 64, UH * u + odd:UH * u + UH:2, :],
                                     qx[64 * odd:64 * odd + 64, u, :, :]).then_inc(s_q4[u], 16)

            for u in range(GU):
                sp.wait_ge(s_ring_out, u + 1)
                spread(0, u)

            def body(p):
                for j in range(SLOTS):
                    if not known(p) or p < PAIRS - 1:
                        for u in units_after(j):
                            sp.wait_ge(s_ring_out, ring_index(p, "g", u) + 1)
                            spread(p, u)
                    if (t := tile_behind(p, j, OUT_AT)) is not None:
                        q, s = t
                        sp.wait_ge(s_out, nkey(q, s, 1))
                        sp.dma_start(out_rows[bass.ds(q * (2 * P) + s * P, P), :], y[:, s, :]).then_inc(s_store[s], 16)

            for p in range(PEELED):
                body(p)
            with sp.Fori(PEELED, PAIRS - 1) as p:
                body(p)
            body(PAIRS - 1)
            body(PAIRS)
            body(PAIRS + 1)
            for s in range(2):
                sp.wait_ge(s_store[s], 16 * PAIRS)

        @block.gpsimd
        def _(pool):
            nc.gpsimd.iota(id_part[:], [[P, 2]], base=0, channel_multiplier=1,
                           allow_small_or_imprecise_dtypes=True).then_inc(s_const, 1)
            nc.gpsimd.iota(id_free[:], [[1, T]], base=0, channel_multiplier=0,
                           allow_small_or_imprecise_dtypes=True).then_inc(s_const, 1)
            nc.gpsimd.memset(ident[:], 0.0).then_inc(s_const, 1)
            nc.gpsimd.memset(ident16[:], 0.0).then_inc(s_const, 1)
            nc.gpsimd.memset(tri[:], 1.0).then_inc(s_const, 1)
            nc.gpsimd.memset(neg_half[:], -0.5).then_inc(s_const, 1)
            pool.wait_ge(s_const, 6)
            nc.gpsimd.affine_select(out=ident[:], in_=ident[:], compare_op=ALU.not_equal, fill=1.0, base=0,
                                    pattern=[[-1, P]], channel_multiplier=1).then_inc(s_const, 1)
            nc.gpsimd.affine_select(out=ident16[:], in_=ident16[:], compare_op=ALU.not_equal, fill=1.0, base=0,
                                    pattern=[[-1, P]], channel_multiplier=1).then_inc(s_const, 1)
            nc.gpsimd.affine_select(out=tri[:], in_=tri[:], compare_op=ALU.is_ge, fill=0.0, base=0,
                                    pattern=[[1, P]], channel_multiplier=-1).then_inc(s_const, 1)
            nc.gpsimd.memset(ones16[:], 1.0).then_inc(s_const, 1)
            nc.gpsimd.memset(amax[:], 0.0).then_inc(s_zero, 1)
            nc.gpsimd.memset(v_rest[:], 0.0).then_inc(s_zero, 1)
            nc.gpsimd.memset(qstack[:, 1], 0.0).then_inc(s_zero, 1)
            pool.wait_ge(s_var0, 2)
            nc.gpsimd.tensor_tensor(rstd0[:, 0:1], var0[:, 0:1], neg_half[:, 0:1], ALU.pow).then_inc(s_rstd0, 1)
            nc.gpsimd.tensor_tensor(rstd0[0:TB, 1:2], var0[0:TB, 1:2], neg_half[0:TB, 0:1], ALU.pow).then_inc(s_rstd0, 1)
            pool.wait_ge(s_ids_col, 16)

            def fetch_ids(q, s):
                nc.gpsimd.tensor_copy(prow_id[:, s:s + 1], ids_col[:, bass.ds(q * 2 + s, 1)]).then_inc(s_pid, 1)

            def fetch(s):
                nc.gpsimd.indirect_dma_start(
                    prow[:, s, :], None, probs_rows[:, :],
                    bass.IndirectOffsetOnAxis(prow_id[:, s:s + 1].bitcast(U32), 0)).then_inc(s_prow[s], 16)

            for s in range(2):
                fetch_ids(0, s)
            pool.wait_ge(s_pdram, 32)
            pool.wait_ge(s_pid, 2)
            for s in range(2):
                fetch(s)
            pool.wait_ge(s_amax, 7)
            nc.gpsimd.partition_all_reduce(gmax[:].rearrange("p a b -> p (a b)"),
                                           amax[:].rearrange("p a b -> p (a b)"), P, ABSMAX).then_inc(s_gmax, 1)
            pool.wait_ge(s_wabs, 1)
            nc.gpsimd.partition_all_reduce(wsum[:], wabs[:], P, RADD).then_inc(s_wsum, 1)
            pool.wait_ge(s_cnt, NT)
            pool.wait_ge(s_bias, 16)

            def body(p):
                for j in range(SLOTS):
                    if (t := group_behind(p, j, LW)) is not None and not by_dve(j - LW):
                        q, jj = t
                        if jj % NG == 0:
                            pool.wait_ge(s_now, nkey(q, jj // NG, 1))
                        weight(pool, nc.gpsimd, q, jj, count_now[:, jj // NG:jj // NG + 1, :], s_wpool)
                    if (t := tile_behind(p, j, N_AT)) is not None:
                        q, s = t
                        pool.wait_ge(s_vs, nkey(q, s, 1))
                        wait(pool, s_xn, nkey(q, s, -1))
                        nc.gpsimd.tensor_tensor(rstd[:, s:s + 1], vs[:, s:s + 1], neg_half[:, 0:1],
                                                ALU.pow).then_inc(s_rstd, 1)
                    if (t := tile_behind(p, j, B_AT)) is not None:
                        q, s = t
                        more = not known(q) or q < PAIRS - 1
                        pool.wait_ge(s_h2, nkey(q, s, 1))
                        if more:
                            fetch_ids(q + 1, s)
                        wait(pool, s_out, nkey(q, s, -1))
                        if more:
                            pool.wait_ge(s_pid, nkey(q, s, 3))
                        nc.gpsimd.tensor_tensor(h2b[:, s, :], h2[:, s, :], bias_b[:], ALU.add).then_inc(s_h2b, 1)
                        if more:
                            fetch(s)

            for p in range(PEELED):
                body(p)
            with pool.Fori(PEELED, PAIRS - 1) as p:
                body(p)
            body(PAIRS - 1)
            body(PAIRS)
            body(PAIRS + 1)

        @block.scalar
        def _(act):
            act.dma_start(ids_row[:], ids_flat.rearrange("(a n) -> a n", a=1).to_broadcast([P, B * S])).then_inc(s_ids_row, 16)
            act.dma_start(wq[:], wq_t.rearrange("(c p) n -> p c n", p=P)).then_inc(s_wq, 16)
            act.dma_start(wp[:], wp_t.rearrange("(c p) n -> p c n", p=P)).then_inc(s_wp, 16)
            for c, n in ((0, P), (1, TB)):
                act.wait_ge(s_nmax, c + 1)
                nc.scalar.activation(probs[0:n, c, :], tbl[0:n, c, :], ACT.Exp, bias=nmax[0:n, c:c + 1],
                                     accum_out=esum[0:n, c:c + 1]).then_inc(s_exp0, 1)
            for half in range(2):
                act.wait_ge(s_lntt_ps, half + 1)
                nc.scalar.copy(lnt_t[:, 2 * half:2 * half + 2, :],
                               tl[half][:, 0:2 * T].rearrange("p (c t) -> p c t", t=T)).then_inc(s_lntt, 1)
            for c in range(TPB):
                for b2 in range(2):
                    e = 2 * c + b2
                    act.wait_ge(s_cnt_ps, e + 1)
                    for b in range(2):
                        nc.scalar.copy(count[:, (2 * b2 + b) * TPB + c, :],
                                       tl[e % 2][:, b * T:b * T + T]).then_inc(s_cnt, 1)
                if c == 0:
                    act.wait_ge(s_zero, 3)
                    for kc, n in ((0, P), (1, TB)):
                        act.wait_ge(s_qs, kc + 1)
                        src = qs[0:n, kc, :].rearrange("p (h d) -> p h d", h=H)
                        nc.scalar.copy(qstack[0:n, kc, :, 0, :], src).then_inc(s_qhi, 1)
                    act.wait_ge(s_ks, 2)
                    nc.scalar.copy(khi[:], ks[:]).then_inc(s_khi, 1)

            def evacuate_gather(u, bank):
                nc.scalar.copy(qx[:, u, :, :], bank[:].rearrange("p (v i) -> p v i", v=2)).then_inc(s_ring_out, 1)

            for u in range(GU):
                act.wait_ge(s_ring_in, u + 1)
                evacuate_gather(u, ring[u % 2])
            act.wait_ge(s_wps, 1)
            nc.scalar.copy(wp_hi, wp_s[:]).then_inc(s_wphi, 1)
            act.wait_ge(s_down, 1)
            unscale = act.alloc_register("unscale")
            act.reg_load(unscale, down[0:1, 0:1].bitcast(I32))

            def body(p):
                for j in range(SLOTS):
                    if (t := group_behind(p, j, LT)) is not None:
                        q, jj = t
                        act.wait_ge(s_ring_in, ring_index(p, "t", j) + 1)
                        wait(act, s_av, gkey(q, jj, 1 - NWT))
                        used = (HG + 1 if len(heads[jj % NG]) == HG else 2) * P
                        nc.scalar.copy(WT[:, jj % NWT, 0:used // P, :], bank_at(p, "t", j)[:, 0:used].rearrange(
                            "p (a i) -> p a i", i=P)).then_inc(s_ring_out, 1)
                    if not known(p) or p < PAIRS - 1:
                        for u in units_after(j):
                            act.wait_ge(s_ring_in, ring_index(p, "g", u) + 1)
                            act.wait_ge(s_q4[u], p * 64 + 64)
                            evacuate_gather(u, bank_at(p, "g", u))
                    if group_behind(p, j, 0) is not None:
                        n = len(heads[j % NG])
                        act.wait_ge(s_nb, gkey(p, j, 1))
                        if not known(p) or gkey(p, j) >= NW:
                            wait_weighted(act, p + (j - NW) // SLOTS, (j - NW) % SLOTS)
                        for a in range(n):
                            ex = nc.scalar.activation(W[:, j % NW, a, :], sc[j % 2][:, a * T:a * T + T], ACT.Exp,
                                                      bias=nb[:, j % 4, a:a + 1], scale=unscale)
                        ex.then_inc(s_e, 1)
                    if (t := tile_behind(p, j, OT_AT)) is not None:
                        q, s = t
                        act.wait_ge(s_ot, nkey(q, s, 1))
                        wait(act, s_h, nkey(q, s, -1))
                        nc.scalar.copy(o_hi[:, s], tl[s][:].rearrange("p (c i) -> p c i", c=KC)).then_inc(s_ohi, 1)
                    if (t := tile_behind(p, j, XT_AT)) is not None:
                        q, s = t
                        act.wait_ge(s_xt, nkey(q, s, 1))
                        wait(act, s_y, nkey(q, s, -1))
                        nc.scalar.copy(x_hi[:, s], tl[s][:].rearrange("p (c i) -> p c i", c=KC)).then_inc(s_xhi, 1)

            for p in range(PEELED):
                body(p)
            with act.Fori(PEELED, PAIRS - 1) as p:
                body(p)
            body(PAIRS - 1)
            body(PAIRS)
            body(PAIRS + 1)

        @block.vector
        def _(dve):
            dve.wait_ge(s_tbl, 32)
            for c, n in ((0, P), (1, TB)):
                nc.vector.tensor_reduce(nmax[0:n, c:c + 1], tbl[0:n, c, :], AX.X, ALU.max,
                                        negate=True).then_inc(s_nmax, 1)
            for c, n in ((0, P), (1, TB)):
                dve.wait_ge(s_exp0, c + 1)
                nc.vector.reciprocal(rsum[0:n, c:c + 1], esum[0:n, c:c + 1]).then_inc(s_rsum, 1)
                dve.wait_ge(s_rsum, c + 1)
                nc.vector.tensor_scalar(probs[0:n, c, :], probs[0:n, c, :], rsum[0:n, c:c + 1], None,
                                        ALU.mult).then_inc(s_probs, 1)
            for c, n in ((0, P), (1, TB)):
                dve.wait_ge(s_probs, c + 1)
                nc.vector.bn_stats(st0[0:n, c, :], probs[0:n, c, :]).then_inc(s_st0, 1)
                dve.wait_ge(s_st0, 2 * c + 1)
                nc.vector.bn_aggr(mv0[0:n, c, :], st0[0:n, c, :]).then_inc(s_st0, 1)
                dve.wait_ge(s_st0, 2 * c + 2)
                nc.vector.tensor_scalar(var0[0:n, c:c + 1], mv0[0:n, c, 1:2], LN_EPS, None, ALU.add).then_inc(s_var0, 1)
            dve.wait_ge(s_ids_col, 16)
            dve.wait_ge(s_const, 10)
            nc.vector.tensor_tensor(
                oh_col[:].rearrange("p b c t -> p (b c) t"), ids_col[:].unsqueeze(2).to_broadcast([P, NT, T]),
                id_free[:].unsqueeze(1).to_broadcast([P, NT, T]), ALU.is_equal).then_inc(s_ohcol, 1)
            for c, n in ((0, P), (1, TB)):
                dve.wait_ge(s_rstd0, c + 1)
                nc.vector.tensor_scalar(lnt[0:n, c, :], probs[0:n, c, :], mv0[0:n, c, 0:1], rstd0[0:n, c:c + 1],
                                        ALU.subtract, ALU.mult).then_inc(s_lnt, 1)
            dve.wait_ge(s_ohcol, 1)
            nc.vector.tensor_copy(oh_sum[:, :, 1, :], oh_col[:, :, 0, :]).then_inc(s_ohsum, 1)
            for c in range(2, TPB):
                dve.wait_ge(s_ohsum, c - 1)
                nc.vector.tensor_tensor(oh_sum[:, :, c, :], oh_sum[:, :, c - 1, :], oh_col[:, :, c - 1, :],
                                        ALU.add).then_inc(s_ohsum, 1)
            dve.wait_ge(s_ids_row, 16)
            for c in range(2):
                nc.vector.tensor_scalar(oh_row[:, c, :], ids_row[:], id_part[:, c:c + 1], None,
                                        ALU.is_equal).then_inc(s_ohrow, 1)
            dve.wait_ge(s_zero, 1)
            for c in range(2):
                dve.wait_ge(s_k_ps, c + 1)
                nc.vector.tensor_reduce(amax[:, 1, c:c + 1], av[c][:, 0:2 * T], AX.X, ALU.max,
                                        apply_absolute_value=True).then_inc(s_amax, 1)
            for c, n in ((0, P), (1, TB)):
                dve.wait_ge(s_q_ps, c + 1)
                nc.vector.tensor_reduce(amax[0:n, 0, c:c + 1], sc[c][0:n, :], AX.X, ALU.max,
                                        apply_absolute_value=True).then_inc(s_amax, 1)
            for c, n in ((0, P), (1, TB)):
                dve.wait_ge(s_v_ps, c + 1)
                nc.vector.tensor_reduce(amax[0:n, 2, c:c + 1], ring[c][0:n, :], AX.X, ALU.max,
                                        apply_absolute_value=True).then_inc(s_amax, 1)
            dve.wait_ge(s_wp, 16)
            nc.vector.tensor_reduce(amax[:, 3, 0:1], wp[:].rearrange("p c n -> p (c n)"), AX.X, ALU.max,
                                    apply_absolute_value=True).then_inc(s_amax, 1)
            dve.wait_ge(s_gmax, 1)
            nc.vector.tensor_reduce(kmax[:], gmax[:], AX.X, ALU.max).then_inc(s_kmax, 1)
            dve.wait_ge(s_kmax, 1)
            nc.vector.tensor_scalar(kmag[:], kmax[:], 1e-18, None, ALU.max).then_inc(s_kmax, 1)
            dve.wait_ge(s_kmax, 2)
            nc.vector.tensor_scalar(power[:].bitcast(U32), kmag[:].bitcast(U32), EXPONENT, None,
                                    ALU.bitwise_and).then_inc(s_kmax, 1)
            nc.vector.tensor_scalar(upinv[:].bitcast(U32), kmag[:].bitcast(U32), EXPONENT, EXPONENT,
                                    ALU.bitwise_and, ALU.bitwise_xor).then_inc(s_kmax, 1)
            dve.wait_ge(s_kmax, 4)
            nc.vector.tensor_scalar(up[:], upinv[:], 4096.0, None, ALU.mult).then_inc(s_up, 1)
            nc.vector.tensor_tensor(downs[:], power[:, 0:4:2], power[:, 1:4:2], ALU.mult).then_inc(s_kmax, 1)
            dve.wait_ge(s_kmax, 5)
            nc.vector.tensor_scalar(down[:, 0:1], downs[:, 0:1], 2.0 ** -26, INV_SQRT, ALU.mult, ALU.mult)
            nc.vector.tensor_scalar(down[:, 1:2], downs[:, 1:2], 2.0 ** -26, None, ALU.mult).then_inc(s_down, 1)
            dve.wait_ge(s_up, 1)
            for kc, n in ((0, P), (1, TB)):
                nc.vector.tensor_scalar(qs[0:n, kc, :], sc[kc][0:n, :], up[0:n, 0:1], None, ALU.mult).then_inc(s_qs, 1)
            for c in range(2):
                nc.vector.tensor_scalar(ks[:, 2 * c:2 * c + 2, :].rearrange("p c t -> p (c t)"), av[c][:, 0:2 * T],
                                        up[:, 1:2], None, ALU.mult).then_inc(s_ks, 1)
            for kc, n in ((0, P), (1, TB)):
                dve.wait_ge(s_qs, kc + 1)
                dve.wait_ge(s_qhi, kc + 1)
                nc.vector.tensor_tensor(qstack[0:n, kc, :, 1, :], qs[0:n, kc, :].rearrange("p (h d) -> p h d", h=H),
                                        qstack[0:n, kc, :, 0, :], ALU.subtract).then_inc(s_qlo, 1)
            dve.wait_ge(s_khi, 1)
            dve.wait_ge(s_ks, 2)
            nc.vector.tensor_tensor(klo[:], ks[:], khi[:], ALU.subtract).then_inc(s_klo, 1)
            nc.vector.tensor_scalar(v_b[:, :, 0:HD], ring[1][0:TB, :].rearrange("p (h d) -> p h d", h=H), up[0:TB, 2:3],
                                    None, ALU.mult).then_inc(s_vb, 1)
            nc.vector.memset(v_b[:, :, HD:V1], 1.0).then_inc(s_vb, 1)
            nc.vector.tensor_scalar(v_a[:, :, 0:HD], ring[0][:].rearrange("p (h d) -> p h d", h=H), up[:, 2:3],
                                    None, ALU.mult).then_inc(s_va, 1)
            nc.vector.memset(v_a[:, :, HD:V1], 1.0).then_inc(s_va, 1)
            dve.wait_ge(s_cnt, NT)
            for half in range(2):
                h = slice(half * NT // 2, (half + 1) * NT // 2)
                nc.vector.tensor_scalar(mask[:, h, :], count[:, h, :], 0.0, NEG, ALU.is_equal, ALU.mult).then_inc(s_mask, 1)
            dve.wait_ge(s_q_ps, 2)
            nc.vector.tensor_scalar(wp_s[:], wp[:], up[:, 3:4], None, ALU.mult).then_inc(s_wps, 1)
            dve.wait_ge(s_wf, 16)
            nc.vector.tensor_reduce(wabs[:], wf[:].rearrange("p c n -> p (c n)"), AX.X, ALU.add,
                                    apply_absolute_value=True).then_inc(s_wabs, 1)
            dve.wait_ge(s_wphi, 1)
            dve.wait_ge(s_wps, 1)
            nc.vector.tensor_tensor(wp_lo, wp_s[:], wp_hi, ALU.subtract).then_inc(s_wplo, 1)
            dve.wait_ge(s_wsum, 1)
            nc.vector.tensor_scalar(thr[:, 0:1], wsum[:], 1.0 / (D * D), None, ALU.mult).then_inc(s_thr, 1)
            dve.wait_ge(s_thr, 1)
            nc.vector.tensor_scalar(thr[:, 1:2], thr[:, 0:1], QUANT_EPS, 0.5, ALU.add, ALU.mult).then_inc(s_thr, 1)
            nc.vector.tensor_scalar(thr[:, 3:4], thr[:, 0:1], 1.0 / X_SCALE, None, ALU.mult).then_inc(s_thr, 1)
            dve.wait_ge(s_thr, 3)
            nc.vector.tensor_scalar(thr[:, 2:3], thr[:, 1:2], -1.0, None, ALU.mult).then_inc(s_thr, 1)
            dve.wait_ge(s_thr, 4)
            nc.vector.tensor_scalar(wneg, wf[:], thr[:, 2:3], None, ALU.is_lt).then_inc(s_wneg, 1)
            dve.wait_ge(s_wneg, 1)
            nc.vector.scalar_tensor_tensor(out=wtern.rearrange("p c n -> p (c n)"),
                                           in0=wf[:].rearrange("p c n -> p (c n)"), scalar=thr[:, 1:2],
                                           in1=wneg.rearrange("p c n -> p (c n)"), op0=ALU.is_gt,
                                           op1=ALU.subtract).then_inc(s_wtern, 1)
            dve.wait_ge(s_down, 1)

            def body(p):
                for j in range(SLOTS):
                    if (t := tile_behind(p, j, OL_AT)) is not None:
                        q, s = t
                        dve.wait_ge(s_ohi, nkey(q, s, 1))
                        wait(dve, s_h, nkey(q, s, -1))
                        nc.vector.tensor_tensor(o_lo[:, s], tl[s][:].rearrange("p (c i) -> p c i", c=KC), o_hi[:, s],
                                                ALU.subtract).then_inc(s_olo, 1)
                    if group_behind(p, j, 0) is not None:
                        n = len(heads[j % NG])
                        dve.wait_ge(s_score, gkey(p, j, 1))
                        nc.vector.tensor_reduce(gm[:, j % 4, 0:n], sc[j % 2][:, 0:n * T].rearrange("p (a t) -> p a t", a=n),
                                                AX.X, ALU.max, negate=True).then_inc(s_gm, 1)
                        dve.wait_ge(s_gm, gkey(p, j, 1))
                        wait(dve, s_e, gkey(p, j, -3))
                        nc.vector.tensor_scalar(nb[:, j % 4, 0:n], gm[:, j % 4, 0:n], down[:, 0:1], None,
                                                ALU.mult).then_inc(s_nb, 1)
                    if j % NG == 0 and group_behind(p, j, 0) is not None:
                        if not known(p) or p > 0:
                            q, jj = p - 1, j + NG - 1
                            wait_weighted(dve, q, jj)
                        nc.vector.tensor_copy(count_now[:, j // NG:j // NG + 1, :],
                                              count[:, bass.ds(p * 2 + j // NG, 1), :]).then_inc(s_now, 1)
                    if (t := group_behind(p, j, LW)) is not None and by_dve(j - LW):
                        q, jj = t
                        weight(dve, nc.vector, q, jj, count[:, bass.ds(q * 2 + jj // NG, 1), :], s_wdve)
                    for b, (h0, h1) in enumerate(((0, HB0), (HB0, H))):
                        if (t := tile_behind(p, j, O_AT[b])) is not None:
                            q, s = t
                            last = NG // 2 - 1 if b == 0 else NG - 1
                            dve.wait_ge(s_av, gkey(q, NG * s + last, 1))
                            a = av[b][:, 0:(h1 - h0) * V1].rearrange("p (h d) -> p h d", d=V1)
                            nc.vector.reciprocal(rden[:, s, h0:h1].unsqueeze(2), a[:, :, HD:V1]).then_inc(s_rden, 1)
                            dve.wait_ge(s_rden, nkey(q, s) * 2 + (b + 1))
                            wait(dve, s_ot, nkey(q, s, -1))
                            nc.vector.tensor_tensor(
                                o32[:, s, HD * h0:HD * h1].rearrange("p (h d) -> p h d", d=HD), a[:, :, 0:HD],
                                rden[:, s, h0:h1].unsqueeze(2).to_broadcast([P, h1 - h0, HD]), ALU.mult).then_inc(s_o, 1)
                    if (t := tile_behind(p, j, N_AT)) is not None:
                        q, s = t
                        dve.wait_ge(s_h, nkey(q, s, 1))
                        dve.wait_ge(s_prow[s], q * 16 + 16)
                        wait(dve, s_h2b, nkey(q, s, -1))
                        nc.vector.scalar_tensor_tensor(out=h2[:, s, :], in0=tl[s][:], scalar=down[:, 1:2],
                                                       in1=prow[:, s, :], op0=ALU.mult, op1=ALU.add).then_inc(s_h2, 1)
                        dve.wait_ge(s_h2, nkey(q, s, 1))
                        nc.vector.bn_stats(st[:, s, :], h2[:, s, :]).then_inc(s_st, 1)
                        dve.wait_ge(s_down, 1)
                        dve.wait_ge(s_st, nkey(q, s, 1))
                        nc.vector.bn_aggr(mv[:, s, :], st[:, s, :]).then_inc(s_mv, 1)
                        dve.wait_ge(s_mv, nkey(q, s, 1))
                        wait(dve, s_rstd, nkey(q, s, -1))
                        nc.vector.tensor_scalar(vs[:, s:s + 1], mv[:, s, 1:2], LN_EPS, X_SCALE ** -2, ALU.add,
                                                ALU.mult).then_inc(s_vs, 1)
                    if (t := tile_behind(p, j, XN_AT)) is not None:
                        q, s = t
                        dve.wait_ge(s_rstd, nkey(q, s, 1))
                        wait(dve, s_xt, nkey(q, s, -1))
                        nc.vector.tensor_scalar(xn[:, s, :], h2[:, s, :], mv[:, s, 0:1], rstd[:, s:s + 1],
                                                ALU.subtract, ALU.mult).then_inc(s_xn, 1)
                    if (t := tile_behind(p, j, XL_AT)) is not None:
                        q, s = t
                        dve.wait_ge(s_xhi, nkey(q, s, 1))
                        wait(dve, s_y, nkey(q, s, -1))
                        nc.vector.tensor_tensor(x_lo[:, s], tl[s][:].rearrange("p (c i) -> p c i", c=KC), x_hi[:, s],
                                                ALU.subtract).then_inc(s_xlo, 1)
                    if (t := tile_behind(p, j, OUT_AT)) is not None:
                        q, s = t
                        dve.wait_ge(s_y, nkey(q, s, 1))
                        dve.wait_ge(s_h2b, nkey(q, s, 1))
                        wait(dve, s_store[s], q * 16)
                        nc.vector.scalar_tensor_tensor(out=y[:, s, :], in0=tl[s][:], scalar=thr[:, 3:4],
                                                       in1=h2b[:, s, :], op0=ALU.mult, op1=ALU.add).then_inc(s_out, 1)

            for p in range(PEELED):
                body(p)
            with dve.Fori(PEELED, PAIRS - 1) as p:
                body(p)
            body(PAIRS - 1)
            body(PAIRS)
            body(PAIRS + 1)

        @block.tensor
        def _(pe):
            pe.wait_ge(s_const, 10)
            pe.wait_ge(s_lnt, 2)
            for half in range(2):
                for c in range(2):
                    cc = 2 * half + c
                    nc.tensor.transpose(tl[half][:, c * T:c * T + P], lnt[:, 0, cc * P:cc * P + P], ident[:])
                    mm = nc.tensor.transpose(tl[half][:, c * T + P:c * T + T], lnt[0:TB, 1, cc * P:cc * P + P],
                                             ident[0:TB, 0:TB])
                mm.then_inc(s_lntt_ps, 1)
            pe.wait_ge(s_lntt, 2)
            pe.wait_ge(s_wk, 16)
            for g in range(KC):
                for c in range(KC):
                    mm = nc.tensor.matmul(av[g // 2][:, (g % 2) * T:(g % 2) * T + T], wk[:, c, g * P:g * P + P],
                                          lnt_t[:, c, :], start=(c == 0), stop=(c == KC - 1), skip_group_check=True)
                if g % 2:
                    mm.then_inc(s_k_ps, 1)
            for w, loaded, banks, made in ((wq, s_wq, sc, s_q_ps), (wv, s_wv, ring, s_v_ps)):
                pe.wait_ge(loaded, 16)
                for kc, (t0, n) in enumerate(((0, P), (P, TB))):
                    for c in range(KC):
                        mm = nc.tensor.matmul(banks[kc][0:n, :], lnt_t[:, c, t0:t0 + n], w[:, c, :],
                                              start=(c == 0), stop=(c == KC - 1))
                    mm.then_inc(made, 1)
            pe.wait_ge(s_ohcol, 1)
            for c in range(TPB):
                if c:
                    pe.wait_ge(s_ohsum, c)
                for b2 in range(2):
                    e = 2 * c + b2
                    wait(pe, s_cnt, 2 * (e - 1))
                    bank = tl[e % 2][:, 0:2 * T].rearrange("p (b t) -> p b t", b=2)
                    mm = nc.tensor.matmul(bank, tri[:], oh_col[:, 2 * b2:2 * b2 + 2, c, :], start=True, stop=(c == 0))
                    if c:
                        mm = nc.tensor.matmul(bank, ones16[:], oh_sum[:, 2 * b2:2 * b2 + 2, c, :],
                                              start=False, stop=True)
                    mm.then_inc(s_cnt_ps, 1)

            def gather(pair, u, bank):
                for v in range(UH // 2):
                    for kc in range(2):
                        rhs = oh_row[:, kc, bass.ds(pair * (2 * P), 2 * P)]
                        mm = nc.tensor.matmul(bank[:, v * 2 * P:(v + 1) * 2 * P],
                                              qstack[:, kc, UH * u + 2 * v:UH * u + 2 * v + 2, :, :].rearrange(
                                                  "p h r d -> p (h r d)"), rhs, start=(kc == 0), stop=(kc == 1))
                mm.then_inc(s_ring_in, 1)

            pe.wait_ge(s_ohrow, 2)
            pe.wait_ge(s_qlo, 2)
            pe.wait_ge(s_qhi, 2)
            pe.wait_ge(s_zero, 3)
            pe.wait_ge(s_va, 2)
            for u in range(GU):
                wait(pe, s_ring_out, u - 1)
                gather(0, u, ring[u % 2])
            pe.wait_ge(s_ks, 2)
            pe.wait_ge(s_mask, 2)
            pe.wait_ge(s_kst, 16 * 16)
            pe.wait_ge(s_vrest, 16 * HG)

            def scores(p, j):
                s, g = j // NG, j % NG
                n = len(heads[g])
                for u in sorted({heads[g][0] // UH, heads[g][-1] // UH}):
                    pe.wait_ge(s_q4[u], p * 64 + 64)
                wait(pe, s_e, gkey(p, j, -1))
                m = mask[:, bass.ds(p * 2 + s, 1), :].to_broadcast([P, n, T])
                nc.tensor.matmul(sc[j % 2][:, 0:n * T], ident16[:], m, start=True, stop=False, skip_group_check=True)
                for a, h in enumerate(heads[g]):
                    mm = nc.tensor.matmul(sc[j % 2][:, a * T:a * T + T], q4[:, h, s * P:s * P + P], kstack[:, h, :],
                                          start=False, stop=(a == n - 1), skip_group_check=True)
                mm.then_inc(s_score, 1)

            def transposes(p, j):
                q, jj = group_behind(p, j, LT)
                n = len(heads[jj % NG])
                e = ring_index(p, "t", j)
                pe.wait_ge(s_ring_out, e - 1)
                wait_weighted(pe, q, jj)
                bank, w = bank_at(p, "t", j), WC[:, jj % NW, :]
                for a in range(n):
                    nc.tensor.transpose(bank[:, a * P:a * P + P], w[:, a * P:a * P + P], ident[:])
                nc.tensor.transpose(bank[0:n * TB, n * P:n * P + P], w[:, n * P:n * T], ident[:]).then_inc(s_ring_in, 1)

            def attend(q, jj):
                s, g = jj // NG, jj % NG
                n = len(heads[g])
                pe.wait_ge(s_ring_out, ring_of_group(q, jj) + 1)
                b = 0 if heads[g][0] < HB0 else 1
                if heads[g][0] in (0, HB0):
                    wait(pe, s_o, nkey(q, s) * 2 + (b - 1))
                first = heads[g][0] in (0, HB0)
                for a, h in enumerate(heads[g]):
                    at = V1 * (h - HB0 * b)
                    nc.tensor.matmul(av[b][:, at:at + V1], WT[:, jj % NWT, a, :], v_a[:, h, :],
                                     start=(first and a == 0), stop=False, skip_group_check=True)
                at = V1 * (heads[g][0] - HB0 * b)
                nc.tensor.matmul(av[b][:, at:at + n * V1], WT[0:n * TB, jj % NWT, n, :], v_rest[0:n * TB, g, 0:n * V1],
                                 start=False, stop=(g in (NG // 2 - 1, NG - 1)), skip_group_check=True).then_inc(s_av, 1)

            def turn(src, s):
                for c in range(KC):
                    mm = nc.tensor.transpose(tl[s][:, c * P:c * P + P], src[:, s, c * P:c * P + P], ident[:])
                return mm

            wp_passes = [(c, a, b) for c in range(KC) for a, b in ((o_hi, wp_hi), (o_hi, wp_lo), (o_lo, wp_hi))]
            wf_passes = [(c, a, wtern) for a in (x_hi, x_lo) for c in range(KC)]

            def project(s, passes, which):
                for i in which:
                    c, a, b = passes[i]
                    mm = nc.tensor.matmul(tl[s][:], a[:, s, c, :], b[:, c, :], start=(i == 0), stop=(i == len(passes) - 1))
                return mm

            def body(p):
                for j in range(SLOTS):
                    if group_behind(p, j, 0) is not None:
                        scores(p, j)
                    if group_behind(p, j, LT) is not None:
                        transposes(p, j)
                    if (t := group_behind(p, j, LA)) is not None:
                        attend(*t)
                    if not known(p) or p < PAIRS - 1:
                        for u in units_after(j):
                            pe.wait_ge(s_ring_out, ring_index(p, "g", u) - 1)
                            gather(p + 1, u, bank_at(p, "g", u))
                    if (t := tile_behind(p, j, OT_AT)) is not None:
                        q, s = t
                        pe.wait_ge(s_o, nkey(q, s) * 2 + 2)
                        wait(pe, s_out, nkey(q, s, -1))
                        turn(o32, s).then_inc(s_ot, 1)
                    for at, which in H_AT.items():
                        if (t := tile_behind(p, j, at)) is not None:
                            q, s = t
                            if which[0] == 0:
                                pe.wait_ge(s_olo, nkey(q, s, 1))
                                if known(q) and q == 0:
                                    pe.wait_ge(s_wplo, 1)
                            mm = project(s, wp_passes, which)
                            if which[-1] == len(wp_passes) - 1:
                                mm.then_inc(s_h, 1)
                    if (t := tile_behind(p, j, XT_AT)) is not None:
                        q, s = t
                        pe.wait_ge(s_xn, nkey(q, s, 1))
                        turn(xn, s).then_inc(s_xt, 1)
                    for at, which in Y_AT.items():
                        if (t := tile_behind(p, j, at)) is not None:
                            q, s = t
                            if which[0] == 0:
                                pe.wait_ge(s_xlo, nkey(q, s, 1))
                                if known(q) and q == 0:
                                    pe.wait_ge(s_wtern, 1)
                            mm = project(s, wf_passes, which)
                            if which[-1] == len(wf_passes) - 1:
                                mm.then_inc(s_y, 1)

            for p in range(PEELED):
                body(p)
            with pe.Fori(PEELED, PAIRS - 1) as p:
                body(p)
            body(PAIRS - 1)
            body(PAIRS)
            body(PAIRS + 1)


def kernel(x, L0_tok_catid_time_matrix, L0_attn_Wq, L0_attn_Wk, L0_attn_Wv, L0_attn_Wp, L0_ffn_weight, L0_ffn_bias):
    import numpy as np
    import concourse.bacc as bacc
    from concourse.bass_utils import run_bass_kernel_spmd

    nc = bacc.Bacc("TRN2", target_bir_lowering=False, num_devices=1)
    arrays = {
        "ids": np.ascontiguousarray(x),
        "table": np.ascontiguousarray(L0_tok_catid_time_matrix),
        "wq_t": np.ascontiguousarray(np.asarray(L0_attn_Wq).T),
        "wk_t": np.ascontiguousarray(np.asarray(L0_attn_Wk).T),
        "wv_t": np.ascontiguousarray(np.asarray(L0_attn_Wv).T),
        "wp_t": np.ascontiguousarray(np.asarray(L0_attn_Wp).T),
        "wf_t": np.ascontiguousarray(np.asarray(L0_ffn_weight).T),
        "bias": np.ascontiguousarray(L0_ffn_bias),
    }
    args = [nc.dram_tensor(n, a.shape, mybir.dt.from_np(a.dtype), kind="ExternalInput").ap() for n, a in arrays.items()]
    shape = (*arrays["ids"].shape, arrays["table"].shape[1])
    out = nc.dram_tensor("out", shape, F32, kind="ExternalOutput").ap()
    scratch = nc.dram_tensor("probs_by_id", arrays["table"].shape, F32, kind="Internal").ap()
    lm_tower_kernel(nc, *args, out, scratch)
    result = run_bass_kernel_spmd(nc, [arrays], core_ids=[0])
    return result.results[0]["out"]
```

```python
from contextlib import ExitStack

import concourse.bass as bass
from concourse import mybir

ALU = mybir.AluOpType
ACT = mybir.ActivationFunctionType
AX = mybir.AxisListType
F32 = mybir.dt.float32
F16 = mybir.dt.float16
BF16 = mybir.dt.bfloat16
I32 = mybir.dt.int32
U32 = mybir.dt.uint32
ABSMAX = bass.bass_isa.ReduceOp.absmax
RADD = bass.bass_isa.ReduceOp.add

P = 128
LN_EPS = 1e-5
QUANT_EPS = 1e-10
NEG = -1e30
EXPONENT = 0x7F800000
X_SCALE = 1024.0


def lm_tower_kernel(nc, ids, table, wq_t, wk_t, wv_t, wp_t, wf_t, bias, out, probs_dram):
    B, S = ids.shape
    T, D = table.shape
    H = 16
    HD = D // H
    TB = T - P
    NT = B * S // P
    TPB = S // P
    PAIRS = NT // 2
    KC = D // P
    HG = 3
    NG = -(-H // HG)
    SLOTS = 2 * NG
    UH = 4
    GU = H // UH
    heads = [list(range(HG * g, min(HG * g + HG, H))) for g in range(NG)]
    HB0 = HG * (NG // 2)
    V1 = HD + 1
    LW, LT, LA = 1, 3, 4
    O_AT = (LA + NG - 1, LA + NG)
    OT_AT = O_AT[1] + 2
    OL_AT = OT_AT + 1
    H_AT = {OL_AT + 1: range(0, 4), OL_AT + 2: range(4, 12)}
    N_AT = OL_AT + 3
    ST_AT = N_AT + 1
    XN_AT = ST_AT + 1
    XT_AT = XN_AT + 1
    XL_AT = XT_AT + 1
    Y_AT = {XL_AT + 2: range(0, 8)}
    B_AT = XL_AT + 1
    OUT_AT = XL_AT + 3
    WP_AT = (0, 6)
    MASK_AT = ((1, 0), (1, 2), (2, 0))
    KLO_BY_POOL = [(2, 2), (2, 3), (3, 0), (3, 1), (3, 2), (3, 3)]
    COUNTS_AHEAD = 8
    COUNTS_BEFORE_Q = 10
    G_AT = (7, 9, 10, 11)
    PEELED = 3
    INV_SQRT = float(HD) ** -0.5

    ctx = ExitStack()
    with ctx:
        def sb(name, shape, dt):
            return ctx.enter_context(nc.sbuf_tensor(name, shape, dt))

        def sem(name):
            return ctx.enter_context(nc.semaphore(name))

        def pb(name):
            return ctx.enter_context(nc.psum_tensor(name, [P, 512], F32))

        tbl = sb("tbl", [P, 2, D], F32)
        wq = sb("wq", [P, KC, D], F32)
        wk = sb("wk", [P, KC, D], F32)
        wv = sb("wv", [P, KC, D], F32)
        wp = sb("wp", [P, KC, D], F32)
        wf = sb("wf", [P, KC, D], F32)
        ids_row = sb("ids_row", [P, B * S], I32)
        ids_col = sb("ids_col", [P, NT], I32)
        bias_b = sb("bias_b", [P, D], F32)
        id_free = sb("id_free", [P, T], F32)
        id_part = sb("id_part", [P, 2], F32)
        ident = sb("ident", [P, P], F32)
        ident16 = sb("ident16", [P, P], BF16)
        tri = sb("tri", [P, P], F16)
        ones16 = sb("ones16", [P, P], F16)
        neg_half = sb("neg_half", [P, 2], F32)
        nmax = sb("nmax", [P, 2], F32)
        esum = sb("esum", [P, 2], F32)
        rsum = sb("rsum", [P, 2], F32)
        probs = sb("probs", [P, 2, D], F32)
        st0 = sb("st0", [P, 2, 6], F32)
        mv0 = sb("mv0", [P, 2, 2], F32)
        var0 = sb("var0", [P, 2], F32)
        rstd0 = sb("rstd0", [P, 2], F32)
        lnt = sb("lnt", [P, 2, D], F32)
        lnt_t = sb("lnt_t", [P, KC, T], F32)
        amax = sb("amax", [P, 4, 2], F32)
        gmax = sb("gmax", [P, 4, 2], F32)
        kmax = sb("kmax", [P, 4], F32)
        kmag = sb("kmag", [P, 4], F32)
        power = sb("power", [P, 4], F32)
        upinv = sb("upinv", [P, 4], F32)
        up = sb("up", [P, 4], F32)
        down = sb("down", [P, 2], F32)
        downs = sb("downs", [P, 2], F32)
        qs = sb("qs", [P, 2, D], F32)
        qstack = sb("qstack", [P, 2, H, 2, HD], F16)
        ks = sb("ks", [P, KC, T], F32)
        khi = sb("khi", [P, KC, T], F16)
        klo = sb("klo", [P, KC, T], F16)
        kstack = sb("kstack", [P, H, T], F16)
        v_a = sb("v_a", [P, H, V1], F32)
        v_b = sb("v_b", [TB, H, V1], F32)
        v_rest = sb("v_rest", [HG * TB, NG, HG * V1], F32)
        packed = ids_row[:].bitcast(F16).rearrange("p (w c n) -> p w c n", w=4, c=KC)
        wp_hi, wp_lo, wneg, wtern = (packed[:, i] for i in range(4))
        wabs = sb("wabs", [P, 1], F32)
        wsum = sb("wsum", [P, 1], F32)
        thr = sb("thr", [P, 4], F32)
        oh_row = sb("oh_row", [P, 2, B * S], F16)
        oh_col = sb("oh_col", [P, B, TPB, T], F16)
        oh_sum = sb("oh_sum", [P, B, TPB, T], F16)
        count = sb("count", [P, NT, T], F32)
        mask = sb("mask", [P, NT, T], BF16)
        mask_now = sb("mask_now", [P, 2, T], BF16)
        NW, NWT = 3, 3
        qx = sb("qx", [P, GU, 2, 2 * P], F16)
        q4 = sb("q4", [P, H, 2 * P], F16)
        nb = sb("nb", [P, 4, HG], F32)
        count_now = sb("count_now", [P, 2, T], F32)
        W = sb("W", [P, NW, HG, T], F32)
        WC = sb("WC", [P, NW, HG * T], F32)
        WT = sb("WT", [P, NWT, 4, P], F32)
        rden = sb("rden", [P, 2, H], F32)
        o32 = wk[:, 0:2, :]
        parts = oh_sum[:].rearrange("p b c t -> p (b c t)")[:, 0:8 * D].rearrange(
            "p (w s c i) -> p w s c i", w=4, s=2, c=KC)
        o_hi, o_lo, x_hi, x_lo = (parts[:, i] for i in range(4))
        prow = lnt
        prow_id = sb("prow_id", [P, 2], I32)
        h2 = wv[:, 2:4, :]
        h2b = tbl
        st = sb("st", [P, 2, 6], F32)
        mv = sb("mv", [P, 2, 2], F32)
        vs = sb("vs", [P, 2], F32)
        rstd = sb("rstd", [P, 2], F32)
        xn = wk[:, 2:4, :]
        y = wv[:, 0:2, :]

        sc = [pb("sc0"), pb("sc1")]
        ring = [pb("ring0"), pb("ring1")]
        av = [pb("av0"), pb("av1")]
        tl = [pb("tl0"), pb("tl1")]

        s_tbl, s_ids_row, s_ids_col, s_bias = sem("tbl_in"), sem("ids_row_in"), sem("ids_col_in"), sem("bias_in")
        s_wq, s_wk, s_wv, s_wp, s_wf = (sem(f"w{n}_in") for n in "qkvpf")
        s_const, s_zero, s_nmax, s_exp0, s_rsum = (sem(n) for n in ("const_set", "zero_set", "nmax_set", "exp0_done", "rsum_set"))
        s_probs, s_pdram, s_st0, s_var0, s_rstd0, s_lnt = (sem(n) for n in ("probs_set", "probs_stored", "st0_set", "var0_set", "rstd0_set", "lnt_set"))
        s_lntt_ps, s_lntt, s_q_ps, s_k_ps, s_v_ps = (sem(n) for n in ("lntT_psum", "lntT_set", "q_psum", "k_psum", "v_psum"))
        s_amax, s_gmax, s_kmax, s_up, s_downs, s_down = (sem(n) for n in ("amax_set", "gmax_set", "kmax_set", "up_set", "downs_set", "down_set"))
        s_qs, s_qhi, s_qlo = (sem(n) for n in ("qs_set", "qhi_set", "qlo_set"))
        s_ks, s_khi, s_klo, s_kst, s_kst_pool = (sem(n) for n in ("ks_set", "khi_set", "klo_set", "kstack_in", "kstack_in_by_pool"))
        s_va, s_vb, s_vrest = (sem(n) for n in ("va_set", "vb_set", "vrest_in"))
        s_wphi, s_wplo = (sem(n) for n in ("wphi_set", "wplo_set"))
        s_wabs, s_wsum, s_thr, s_wneg, s_wtern = (sem(n) for n in ("wabs_set", "wsum_set", "thr_set", "wneg_set", "wtern_set"))
        s_ohrow, s_ohcol, s_ohsum, s_cnt_ps, s_cnt, s_mask = (sem(n) for n in ("ohrow_set", "ohcol_set", "ohsum_set", "count_psum", "count_set", "mask_set"))
        s_ring_zero, s_ring_in, s_ring_out = sem("ring_zero"), sem("ring_filled"), sem("ring_evacuated")
        s_score, s_nb, s_e = (sem(n) for n in ("scores_ready", "shift_ready", "exp_ready"))
        s_weighted = sem("weighted")
        s_q4 = [sem(f"q4_in{u}") for u in range(GU)]
        s_av, s_now, s_mnow = sem("attended"), sem("count_now_set"), sem("mask_now_set")
        s_rden, s_o, s_ot, s_ohi, s_olo = (sem(n) for n in ("rden_set", "o_ready", "oT_psum", "ohi_ready", "olo_ready"))
        s_h, s_h2, s_st, s_mv, s_vs, s_rstd, s_h2b = (sem(n) for n in ("h_psum", "h2_ready", "stats_ready", "meanvar_ready", "varscaled", "rstd_ready", "h2b_ready"))
        s_xn, s_xt, s_xhi, s_xlo, s_y, s_out = (sem(n) for n in ("xn_ready", "xT_psum", "xhi_ready", "xlo_ready", "y_psum", "out_ready"))
        s_pid, s_prow, s_store = sem("prow_id_set"), [sem("prow_in0"), sem("prow_in1")], [sem("stored0"), sem("stored1")]

        probs_rows = probs_dram
        out_rows = out.rearrange("b (n p) d -> (b n p) d", p=P)
        ids_flat = ids.rearrange("b s -> (b s)")

        def known(p):
            return p.__class__ is int

        def group_behind(p, j, lag):
            back = (j - lag) // SLOTS
            q, jj = p + back, (j - lag) % SLOTS
            if known(p) and not 0 <= q < PAIRS:
                return None
            return q, jj

        def tile_behind(p, j, at):
            if (j - at) % NG:
                return None
            d = (j - at) // NG
            q, s = p + d // 2, d % 2
            if known(p) and not 0 <= q < PAIRS:
                return None
            return q, s

        def gkey(p, j, more=0):
            return p * SLOTS + (j + more)

        def nkey(p, s, more=0):
            return p * 2 + (s + more)

        def wait(eng, s, value):
            if not known(value) or value > 0:
                eng.wait_ge(s, value)

        assert all(G_AT[u] > NG + (UH * u + UH - 1) // HG - 1 for u in range(GU))

        def units_after(j):
            return [u for u in range(GU) if G_AT[u] == j]

        uses = []
        for j in range(SLOTS):
            uses.append(("t", j))
            uses += [("g", u) for u in units_after(j)]
        PER_PAIR = len(uses)

        def ring_index(p, kind, i):
            if known(p) and p < 0:
                return i
            at = uses.index((kind, i))
            if known(p) and p >= PAIRS - 1:
                lost = (GU if p == PAIRS else 0) + sum(k == "g" for k, _ in uses[:at]) * (p == PAIRS - 1)
                return GU - LT + PER_PAIR * p + at - lost
            return p * PER_PAIR + (GU - LT + at)

        def ring_bank(kind, i):
            return (GU - LT + uses.index((kind, i))) % 2

        def ring_of_group(p, j):
            return ring_index(p + (j + LT) // SLOTS, "t", (j + LT) % SLOTS)

        assert PER_PAIR % 2 == 0

        def bank_at(p, kind, i):
            if known(p):
                return ring[ring_index(p, kind, i) % 2]
            return ring[ring_bank(kind, i)]

        block = ctx.enter_context(nc.Block())

        @block.sync
        def _(sp):
            sp.dma_start(tbl[:, 0, :], table[0:P, :]).then_inc(s_tbl, 16)
            sp.dma_start(tbl[0:TB, 1, :], table[P:T, :]).then_inc(s_tbl, 16)
            sp.dma_start(ids_col[:], ids_flat.rearrange("(n p) -> p n", p=P), allow_slow_non_contiguous=True).then_inc(s_ids_col, 16)
            sp.dma_start(wk[:], wk_t.rearrange("(c p) n -> p c n", p=P)).then_inc(s_wk, 16)
            sp.dma_start(ids_row[:], ids_flat.rearrange("(a n) -> a n", a=1).to_broadcast([P, B * S])).then_inc(s_ids_row, 16)
            sp.dma_start(wq[:], wq_t.rearrange("(c p) n -> p c n", p=P)).then_inc(s_wq, 16)
            sp.dma_start(wv[:], wv_t.rearrange("(c p) n -> p c n", p=P)).then_inc(s_wv, 16)
            sp.wait_ge(s_probs, 2)
            sp.dma_start(probs_rows[0:P, :], probs[:, 0, :]).then_inc(s_pdram, 16)
            sp.dma_start(probs_rows[P:T, :], probs[0:TB, 1, :]).then_inc(s_pdram, 16)
            sp.dma_start(wp[:], wp_t.rearrange("(c p) n -> p c n", p=P)).then_inc(s_wp, 16)
            sp.dma_start(wf[:], wf_t.rearrange("(c p) n -> p c n", p=P)).then_inc(s_wf, 16)
            sp.dma_start(bias_b[:], bias.rearrange("(a d) -> a d", a=1).to_broadcast([P, D])).then_inc(s_bias, 16)
            sp.wait_ge(s_khi, 1)
            for r in (0, 1):
                for a in range(4):
                    sp.dma_start(kstack[HD * r:HD * r + HD, a::4, :], khi[HD * a:HD * a + HD, :, :]).then_inc(s_kst, 16)
            sp.wait_ge(s_klo, 1)
            for r in (2, 3):
                for a in range(4):
                    if (r, a) not in KLO_BY_POOL:
                        sp.dma_start(kstack[HD * r:HD * r + HD, a::4, :], klo[HD * a:HD * a + HD, :, :]).then_inc(s_kst, 16)

            def spread(p, u):
                for odd in range(2):
                    for half in range(2):
                        sp.dma_start(q4[64 * half:64 * half + 64, UH * u + odd:UH * u + UH:2, :],
                                     qx[64 * odd:64 * odd + 64, u, :, :]).then_inc(s_q4[u], 16)

            for u in range(GU):
                sp.wait_ge(s_ring_out, u + 1)
                spread(0, u)
            sp.wait_ge(s_vb, 2)
            sp.wait_ge(s_zero, 2)
            for a in range(HG):
                n = len(range(a, H, HG))
                sp.dma_start(v_rest[TB * a:TB * a + TB, 0:n, V1 * a:V1 * a + V1], v_b[:, a::HG, :]).then_inc(s_vrest, 16)

            def body(p):
                for j in range(SLOTS):
                    if not known(p) or p < PAIRS - 1:
                        for u in units_after(j):
                            sp.wait_ge(s_ring_out, ring_index(p, "g", u) + 1)
                            spread(p, u)
                    if (t := tile_behind(p, j, OUT_AT)) is not None:
                        q, s = t
                        sp.wait_ge(s_out, nkey(q, s, 1))
                        sp.dma_start(out_rows[bass.ds(q * (2 * P) + s * P, P), :], y[:, s, :]).then_inc(s_store[s], 16)

            for p in range(PEELED):
                body(p)
            with sp.Fori(PEELED, PAIRS - 1) as p:
                body(p)
            body(PAIRS - 1)
            body(PAIRS)
            body(PAIRS + 1)
            for s in range(2):
                sp.wait_ge(s_store[s], 16 * PAIRS)

        @block.gpsimd
        def _(pool):
            nc.gpsimd.iota(id_part[:], [[P, 2]], base=0, channel_multiplier=1,
                           allow_small_or_imprecise_dtypes=True).then_inc(s_const, 1)
            nc.gpsimd.iota(id_free[:], [[1, T]], base=0, channel_multiplier=0,
                           allow_small_or_imprecise_dtypes=True).then_inc(s_const, 1)
            nc.gpsimd.memset(ident[:], 0.0).then_inc(s_const, 1)
            nc.gpsimd.memset(ident16[:], 0.0).then_inc(s_const, 1)
            nc.gpsimd.memset(tri[:], 1.0).then_inc(s_const, 1)
            nc.gpsimd.memset(neg_half[:], -0.5).then_inc(s_const, 1)
            pool.wait_ge(s_const, 6)
            nc.gpsimd.affine_select(out=ident[:], in_=ident[:], compare_op=ALU.not_equal, fill=1.0, base=0,
                                    pattern=[[-1, P]], channel_multiplier=1).then_inc(s_const, 1)
            nc.gpsimd.affine_select(out=ident16[:], in_=ident16[:], compare_op=ALU.not_equal, fill=1.0, base=0,
                                    pattern=[[-1, P]], channel_multiplier=1).then_inc(s_const, 1)
            nc.gpsimd.affine_select(out=tri[:], in_=tri[:], compare_op=ALU.is_ge, fill=0.0, base=0,
                                    pattern=[[1, P]], channel_multiplier=-1).then_inc(s_const, 1)
            nc.gpsimd.memset(ones16[:], 1.0).then_inc(s_const, 1)
            nc.gpsimd.memset(amax[:], 0.0).then_inc(s_zero, 1)
            nc.gpsimd.memset(v_rest[:], 0.0).then_inc(s_zero, 1)
            nc.gpsimd.memset(qstack[:, 1], 0.0).then_inc(s_zero, 1)
            pool.wait_ge(s_var0, 2)
            nc.gpsimd.tensor_tensor(rstd0[:, 0:1], var0[:, 0:1], neg_half[:, 0:1], ALU.pow).then_inc(s_rstd0, 1)
            nc.gpsimd.tensor_tensor(rstd0[0:TB, 1:2], var0[0:TB, 1:2], neg_half[0:TB, 0:1], ALU.pow).then_inc(s_rstd0, 1)
            pool.wait_ge(s_ids_col, 16)

            def fetch_ids(q, s):
                nc.gpsimd.tensor_copy(prow_id[:, s:s + 1], ids_col[:, bass.ds(q * 2 + s, 1)]).then_inc(s_pid, 1)

            def fetch(s):
                nc.gpsimd.indirect_dma_start(
                    prow[:, s, :], None, probs_rows[:, :],
                    bass.IndirectOffsetOnAxis(prow_id[:, s:s + 1].bitcast(U32), 0)).then_inc(s_prow[s], 16)

            for s in range(2):
                fetch_ids(0, s)
            pool.wait_ge(s_lntt_ps, 2)
            pool.wait_ge(s_pdram, 32)
            pool.wait_ge(s_pid, 2)
            for s in range(2):
                fetch(s)
            def reduce_amax(w0, w1):
                nc.gpsimd.partition_all_reduce(gmax[:, w0:w1, :].rearrange("p a b -> p (a b)"),
                                               amax[:, w0:w1, :].rearrange("p a b -> p (a b)"), P, ABSMAX).then_inc(s_gmax, 1)

            pool.wait_ge(s_amax, 5)
            reduce_amax(0, 3)
            pool.wait_ge(s_wabs, 1)
            nc.gpsimd.partition_all_reduce(wsum[:], wabs[:], P, RADD).then_inc(s_wsum, 1)
            pool.wait_ge(s_klo, 1)
            for r, a in KLO_BY_POOL:
                nc.gpsimd.dma_start(kstack[HD * r:HD * r + HD, a::4, :], klo[HD * a:HD * a + HD, :, :]).then_inc(s_kst_pool, 16)
            pool.wait_ge(s_amax, 7)
            reduce_amax(3, 4)
            pool.wait_ge(s_bias, 16)

            def weight(q, jj):
                n = len(heads[jj % NG])
                pool.wait_ge(s_e, gkey(q, jj, 1))
                if not known(q) or gkey(q, jj) >= NW:
                    pool.wait_ge(s_ring_in, ring_of_group(q + (jj - NW) // SLOTS, (jj - NW) % SLOTS) + 1)
                w, c = W[:, jj % NW, 0:n, :], count_now[:, jj // NG:jj // NG + 1, :]
                wide = WC[:, jj % NW, 0:n * P].rearrange("p (a t) -> p a t", a=n)
                rest = WC[:, jj % NW, n * P:n * T].rearrange("p (a t) -> p a t", a=n)
                nc.gpsimd.tensor_tensor(wide, w[:, :, 0:P], c[:, :, 0:P].to_broadcast([P, n, P]),
                                        ALU.mult).then_inc(s_weighted, 1)
                nc.gpsimd.tensor_tensor(rest, w[:, :, P:T], c[:, :, P:T].to_broadcast([P, n, TB]),
                                        ALU.mult).then_inc(s_weighted, 1)

            def body(p):
                for j in range(SLOTS):
                    if (t := group_behind(p, j, LW)) is not None:
                        q, jj = t
                        if jj % NG == 0:
                            pool.wait_ge(s_now, nkey(q, jj // NG, 1))
                        weight(q, jj)
                    if (t := tile_behind(p, j, ST_AT)) is not None:
                        q, s = t
                        pool.wait_ge(s_vs, nkey(q, s, 1))
                        wait(pool, s_xn, nkey(q, s, -1))
                        nc.gpsimd.tensor_tensor(rstd[:, s:s + 1], vs[:, s:s + 1], neg_half[:, 0:1],
                                                ALU.pow).then_inc(s_rstd, 1)
                    if (t := tile_behind(p, j, B_AT)) is not None:
                        q, s = t
                        more = not known(q) or q < PAIRS - 1
                        pool.wait_ge(s_h2, nkey(q, s, 1))
                        if more:
                            fetch_ids(q + 1, s)
                        wait(pool, s_out, nkey(q, s, -1))
                        if more:
                            pool.wait_ge(s_pid, nkey(q, s, 3))
                        nc.gpsimd.tensor_tensor(h2b[:, s, :], h2[:, s, :], bias_b[:], ALU.add).then_inc(s_h2b, 1)
                        if more:
                            fetch(s)

            for p in range(PEELED):
                body(p)
            with pool.Fori(PEELED, PAIRS - 1) as p:
                body(p)
            body(PAIRS - 1)
            body(PAIRS)
            body(PAIRS + 1)

        @block.scalar
        def _(act):
            for c, n in ((0, P), (1, TB)):
                act.wait_ge(s_nmax, c + 1)
                nc.scalar.activation(probs[0:n, c, :], tbl[0:n, c, :], ACT.Exp, bias=nmax[0:n, c:c + 1],
                                     accum_out=esum[0:n, c:c + 1]).then_inc(s_exp0, 1)
            for half in range(2):
                act.wait_ge(s_lntt_ps, half + 1)
                nc.scalar.copy(lnt_t[:, 2 * half:2 * half + 2, :],
                               tl[half][:, 0:2 * T].rearrange("p (c t) -> p c t", t=T)).then_inc(s_lntt, 1)
            def evacuate_counts(e):
                act.wait_ge(s_cnt_ps, e + 1)
                for b in range(2):
                    nc.scalar.copy(count[:, (2 * (e // TPB) + b) * TPB + e % TPB, :],
                                   tl[e % 2][:, b * T:b * T + T]).then_inc(s_cnt, 1)

            for e in range(COUNTS_AHEAD):
                evacuate_counts(e)
            act.wait_ge(s_wf, 16)
            act.wait_ge(s_ohrow, 2)
            nc.scalar.activation(ids_row[:, 0:KC * D].bitcast(F32), wf[:].rearrange("p c n -> p (c n)"), ACT.Abs,
                                 accum_out=wabs[:]).then_inc(s_wabs, 1)
            act.wait_ge(s_zero, 3)
            for kc, n in ((0, P), (1, TB)):
                act.wait_ge(s_qs, kc + 1)
                src = qs[0:n, kc, :].rearrange("p (h d) -> p h d", h=H)
                nc.scalar.copy(qstack[0:n, kc, :, 0, :], src).then_inc(s_qhi, 1)
            act.wait_ge(s_ks, 2)
            nc.scalar.copy(khi[:], ks[:]).then_inc(s_khi, 1)
            for e in range(COUNTS_AHEAD, COUNTS_BEFORE_Q):
                evacuate_counts(e)

            def evacuate_gather(u, bank):
                nc.scalar.copy(qx[:, u, :, :], bank[:].rearrange("p (v i) -> p v i", v=2)).then_inc(s_ring_out, 1)

            for u in range(GU):
                act.wait_ge(s_ring_in, u + 1)
                evacuate_gather(u, sc[u % 2])
            for e in range(COUNTS_BEFORE_Q, 2 * TPB):
                evacuate_counts(e)
            act.wait_ge(s_up, 1)
            act.wait_ge(s_wabs, 1)
            nc.scalar.activation(wp_hi, wp[:], ACT.Copy, scale=up[:, 2:3]).then_inc(s_wphi, 1)

            def body(p):
                for j in range(SLOTS):
                    if (t := group_behind(p, j, LT)) is not None:
                        q, jj = t
                        act.wait_ge(s_ring_in, ring_index(p, "t", j) + 1)
                        wait(act, s_av, gkey(q, jj, 1 - NWT))
                        used = (HG + 1 if len(heads[jj % NG]) == HG else 2) * P
                        nc.scalar.copy(WT[:, jj % NWT, 0:used // P, :], bank_at(p, "t", j)[:, 0:used].rearrange(
                            "p (a i) -> p a i", i=P)).then_inc(s_ring_out, 1)
                    if not known(p) or p < PAIRS - 1:
                        for u in units_after(j):
                            act.wait_ge(s_ring_in, ring_index(p, "g", u) + 1)
                            act.wait_ge(s_q4[u], p * 64 + 64)
                            evacuate_gather(u, bank_at(p, "g", u))
                    if group_behind(p, j, 0) is not None:
                        n = len(heads[j % NG])
                        act.wait_ge(s_nb, gkey(p, j, 1))
                        if not known(p) or gkey(p, j) >= NW:
                            act.wait_ge(s_weighted, gkey(p, j, 1 - NW) * 2)
                        for a in range(n):
                            ex = nc.scalar.activation(W[:, j % NW, a, :], sc[j % 2][:, a * T:a * T + T], ACT.Exp,
                                                      bias=nb[:, j % 4, a:a + 1], scale=-1.0)
                        ex.then_inc(s_e, 1)
                    if (t := tile_behind(p, j, OT_AT)) is not None:
                        q, s = t
                        act.wait_ge(s_ot, nkey(q, s, 1))
                        wait(act, s_h, nkey(q, s, -1))
                        nc.scalar.copy(o_hi[:, s], tl[s][:].rearrange("p (c i) -> p c i", c=KC)).then_inc(s_ohi, 1)
                    if (t := tile_behind(p, j, XT_AT)) is not None:
                        q, s = t
                        act.wait_ge(s_xt, nkey(q, s, 1))
                        wait(act, s_y, nkey(q, s, -1))
                        nc.scalar.copy(x_hi[:, s], tl[s][:].rearrange("p (c i) -> p c i", c=KC)).then_inc(s_xhi, 1)

            for p in range(PEELED):
                body(p)
            with act.Fori(PEELED, PAIRS - 1) as p:
                body(p)
            body(PAIRS - 1)
            body(PAIRS)
            body(PAIRS + 1)

        @block.vector
        def _(dve):
            nc.vector.memset(ring[1][:], 0.0).then_inc(s_ring_zero, 1)
            dve.wait_ge(s_tbl, 32)
            for c, n in ((0, P), (1, TB)):
                nc.vector.tensor_reduce(nmax[0:n, c:c + 1], tbl[0:n, c, :], AX.X, ALU.max,
                                        negate=True).then_inc(s_nmax, 1)
            for c, n in ((0, P), (1, TB)):
                dve.wait_ge(s_exp0, c + 1)
                nc.vector.reciprocal(rsum[0:n, c:c + 1], esum[0:n, c:c + 1]).then_inc(s_rsum, 1)
                dve.wait_ge(s_rsum, c + 1)
                nc.vector.tensor_scalar(probs[0:n, c, :], probs[0:n, c, :], rsum[0:n, c:c + 1], None,
                                        ALU.mult).then_inc(s_probs, 1)
            for c, n in ((0, P), (1, TB)):
                dve.wait_ge(s_probs, c + 1)
                nc.vector.bn_stats(st0[0:n, c, :], probs[0:n, c, :]).then_inc(s_st0, 1)
                dve.wait_ge(s_st0, 2 * c + 1)
                nc.vector.bn_aggr(mv0[0:n, c, :], st0[0:n, c, :]).then_inc(s_st0, 1)
                dve.wait_ge(s_st0, 2 * c + 2)
                nc.vector.tensor_scalar(var0[0:n, c:c + 1], mv0[0:n, c, 1:2], LN_EPS, None, ALU.add).then_inc(s_var0, 1)
            dve.wait_ge(s_ids_col, 16)
            dve.wait_ge(s_const, 10)

            def one_hot(b):
                nc.vector.tensor_tensor(
                    oh_col[:, b], ids_col[:, b * TPB:(b + 1) * TPB].unsqueeze(2).to_broadcast([P, TPB, T]),
                    id_free[:].unsqueeze(1).to_broadcast([P, TPB, T]), ALU.is_equal).then_inc(s_ohcol, 1)

            one_hot(0)
            for c, n in ((0, P), (1, TB)):
                dve.wait_ge(s_rstd0, c + 1)
                nc.vector.tensor_scalar(lnt[0:n, c, :], probs[0:n, c, :], mv0[0:n, c, 0:1], rstd0[0:n, c:c + 1],
                                        ALU.subtract, ALU.mult).then_inc(s_lnt, 1)
            for b in range(1, B):
                one_hot(b)
            dve.wait_ge(s_ohcol, B)
            nc.vector.tensor_copy(oh_sum[:, :, 1, :], oh_col[:, :, 0, :]).then_inc(s_ohsum, 1)
            for c in range(2, TPB):
                dve.wait_ge(s_ohsum, c - 1)
                nc.vector.tensor_tensor(oh_sum[:, :, c, :], oh_sum[:, :, c - 1, :], oh_col[:, :, c - 1, :],
                                        ALU.add).then_inc(s_ohsum, 1)
            dve.wait_ge(s_ids_row, 16)
            for c in range(2):
                nc.vector.tensor_scalar(oh_row[:, c, :], ids_row[:], id_part[:, c:c + 1], None,
                                        ALU.is_equal).then_inc(s_ohrow, 1)
            dve.wait_ge(s_zero, 1)
            for c in range(2):
                dve.wait_ge(s_k_ps, c + 1)
                nc.vector.tensor_reduce(amax[:, 1, c:c + 1], av[c][:, 0:2 * T], AX.X, ALU.max,
                                        apply_absolute_value=True).then_inc(s_amax, 1)
            dve.wait_ge(s_wp, 16)
            nc.vector.tensor_reduce(amax[:, 2, 0:1], wp[:].rearrange("p c n -> p (c n)"), AX.X, ALU.max,
                                    apply_absolute_value=True).then_inc(s_amax, 1)
            for c, n in ((0, P), (1, TB)):
                dve.wait_ge(s_q_ps, c + 1)
                nc.vector.tensor_reduce(amax[0:n, 0, c:c + 1], sc[c][0:n, :], AX.X, ALU.max,
                                        apply_absolute_value=True).then_inc(s_amax, 1)
            def scale_up(i, w0, w1):
                dve.wait_ge(s_gmax, i + 1)
                nc.vector.tensor_reduce(kmax[:, w0:w1], gmax[:, w0:w1, :], AX.X, ALU.max).then_inc(s_kmax, 1)
                dve.wait_ge(s_kmax, 4 * i + 1)
                nc.vector.tensor_scalar(kmag[:, w0:w1], kmax[:, w0:w1], 1e-18, None, ALU.max).then_inc(s_kmax, 1)
                dve.wait_ge(s_kmax, 4 * i + 2)
                nc.vector.tensor_scalar(power[:, w0:w1].bitcast(U32), kmag[:, w0:w1].bitcast(U32), EXPONENT, None,
                                        ALU.bitwise_and).then_inc(s_kmax, 1)
                nc.vector.tensor_scalar(upinv[:, w0:w1].bitcast(U32), kmag[:, w0:w1].bitcast(U32), EXPONENT, EXPONENT,
                                        ALU.bitwise_and, ALU.bitwise_xor).then_inc(s_kmax, 1)
                dve.wait_ge(s_kmax, 4 * i + 4)
                nc.vector.tensor_scalar(up[:, w0:w1], upinv[:, w0:w1], 4096.0, None, ALU.mult).then_inc(s_up, 1)

            scale_up(0, 0, 3)
            nc.vector.tensor_tensor(downs[:, 0:1], power[:, 0:1], power[:, 1:2], ALU.mult).then_inc(s_downs, 1)
            dve.wait_ge(s_downs, 1)
            nc.vector.tensor_scalar(down[:, 0:1], downs[:, 0:1], -2.0 ** -26, INV_SQRT, ALU.mult, ALU.mult).then_inc(s_down, 1)
            dve.wait_ge(s_up, 1)
            for kc, n in ((0, P), (1, TB)):
                nc.vector.tensor_scalar(qs[0:n, kc, :], sc[kc][0:n, :], up[0:n, 0:1], None, ALU.mult).then_inc(s_qs, 1)
            for c in range(2):
                nc.vector.tensor_scalar(ks[:, 2 * c:2 * c + 2, :].rearrange("p c t -> p (c t)"), av[c][:, 0:2 * T],
                                        up[:, 1:2], None, ALU.mult).then_inc(s_ks, 1)
            for kc, n in ((0, P), (1, TB)):
                dve.wait_ge(s_qs, kc + 1)
                dve.wait_ge(s_qhi, kc + 1)
                nc.vector.tensor_tensor(qstack[0:n, kc, :, 1, :], qs[0:n, kc, :].rearrange("p (h d) -> p h d", h=H),
                                        qstack[0:n, kc, :, 0, :], ALU.subtract).then_inc(s_qlo, 1)
            dve.wait_ge(s_khi, 1)
            dve.wait_ge(s_ks, 2)
            nc.vector.tensor_tensor(klo[:], ks[:], khi[:], ALU.subtract).then_inc(s_klo, 1)
            dve.wait_ge(s_wsum, 1)
            nc.vector.tensor_scalar(thr[:, 0:1], wsum[:], 1.0 / (D * D), None, ALU.mult).then_inc(s_thr, 1)
            dve.wait_ge(s_thr, 1)
            nc.vector.tensor_scalar(thr[:, 1:2], thr[:, 0:1], QUANT_EPS, 0.5, ALU.add, ALU.mult).then_inc(s_thr, 1)
            nc.vector.tensor_scalar(thr[:, 3:4], thr[:, 0:1], 1.0 / X_SCALE, None, ALU.mult).then_inc(s_thr, 1)
            dve.wait_ge(s_thr, 3)
            nc.vector.tensor_scalar(thr[:, 2:3], thr[:, 1:2], -1.0, None, ALU.mult).then_inc(s_thr, 1)
            dve.wait_ge(s_thr, 4)
            nc.vector.tensor_scalar(wneg, wf[:], thr[:, 2:3], None, ALU.is_lt).then_inc(s_wneg, 1)
            dve.wait_ge(s_wneg, 1)
            nc.vector.scalar_tensor_tensor(out=wtern.rearrange("p c n -> p (c n)"),
                                           in0=wf[:].rearrange("p c n -> p (c n)"), scalar=thr[:, 1:2],
                                           in1=wneg.rearrange("p c n -> p (c n)"), op0=ALU.is_gt,
                                           op1=ALU.subtract).then_inc(s_wtern, 1)
            dve.wait_ge(s_down, 1)
            for c, n in ((0, P), (1, TB)):
                dve.wait_ge(s_v_ps, c + 1)
                nc.vector.tensor_reduce(amax[0:n, 3, c:c + 1], ring[c][0:n, :], AX.X, ALU.max,
                                        apply_absolute_value=True).then_inc(s_amax, 1)
            scale_up(1, 3, 4)
            dve.wait_ge(s_up, 2)
            nc.vector.tensor_scalar(v_b[:, :, 0:HD], ring[1][0:TB, :].rearrange("p (h d) -> p h d", h=H), up[0:TB, 3:4],
                                    None, ALU.mult).then_inc(s_vb, 1)
            nc.vector.memset(v_b[:, :, HD:V1], 1.0).then_inc(s_vb, 1)
            nc.vector.tensor_scalar(v_a[:, :, 0:HD], ring[0][:].rearrange("p (h d) -> p h d", h=H), up[:, 3:4],
                                    None, ALU.mult).then_inc(s_va, 1)
            nc.vector.memset(v_a[:, :, HD:V1], 1.0).then_inc(s_va, 1)
            dve.wait_ge(s_cnt, 2 * TPB)

            def make_mask(b):
                h = slice(b * TPB, (b + 1) * TPB)
                nc.vector.tensor_scalar(mask[:, h, :], count[:, h, :], 0.0, NEG, ALU.is_equal, ALU.mult).then_inc(s_mask, 1)

            make_mask(0)

            def prepare_wp():
                nc.vector.tensor_tensor(downs[:, 1:2], power[:, 2:3], power[:, 3:4], ALU.mult).then_inc(s_downs, 1)
                dve.wait_ge(s_downs, 2)
                nc.vector.tensor_scalar(down[:, 1:2], downs[:, 1:2], 2.0 ** -26, None, ALU.mult).then_inc(s_down, 1)
                dve.wait_ge(s_wphi, 1)
                nc.vector.scalar_tensor_tensor(out=wp_lo.rearrange("p c n -> p (c n)"),
                                               in0=wp[:].rearrange("p c n -> p (c n)"), scalar=up[:, 2:3],
                                               in1=wp_hi.rearrange("p c n -> p (c n)"), op0=ALU.mult,
                                               op1=ALU.subtract).then_inc(s_wplo, 1)

            scores_out = dve.alloc_register("scores_out")

            def copy_mask(q, s):
                nc.vector.tensor_copy(mask_now[:, s % 2:s % 2 + 1, :],
                                      mask[:, bass.ds(q * 2 + s, 1), :]).then_inc(s_mnow, 1)

            dve.wait_ge(s_mask, 1)
            copy_mask(0, 0)
            dve.wait_ge(s_mnow, 1)

            def body(p):
                for j in range(SLOTS):
                    if group_behind(p, j, 0) is not None:
                        n = len(heads[j % NG])
                        if j % NG == 0:
                            wait(dve, s_mnow, nkey(p, j // NG, 1))
                        if known(p):
                            dve.wait_ge(s_score, gkey(p, j, 1))
                        else:
                            dve.reg_add(scores_out, scores_out, 1)
                            dve.wait_ge(s_down, 1)
                            dve.wait_ge(s_score, scores_out)
                        m = mask_now[:, j // NG, :]
                        for a in range(n):
                            scored = sc[j % 2][:, a * T:a * T + T]
                            mx = nc.vector.tensor_tensor_reduce(scored, scored, m, down[:, 0:1], -NEG, ALU.add, ALU.min,
                                                                nb[:, j % 4, a:a + 1])
                        mx.then_inc(s_nb, 1)
                    if known(p) and (p, j) == WP_AT:
                        prepare_wp()
                    if known(p) and (p, j) in MASK_AT:
                        if MASK_AT[0] != (p, j):
                            dve.wait_ge(s_cnt, NT)
                        make_mask(MASK_AT.index((p, j)) + 1)
                    if j % NG == NG - 2 and group_behind(p, j, -2) is not None:
                        copy_mask(p, j // NG + 1)
                    if j % NG == 0 and group_behind(p, j, 0) is not None:
                        if not known(p) or p > 0:
                            q, jj = p - 1, j + NG - 1
                            dve.wait_ge(s_weighted, gkey(q, jj, 1) * 2)
                        nc.vector.tensor_copy(count_now[:, j // NG:j // NG + 1, :],
                                              count[:, bass.ds(p * 2 + j // NG, 1), :]).then_inc(s_now, 1)
                    for b, (h0, h1) in enumerate(((0, HB0), (HB0, H))):
                        if (t := tile_behind(p, j, O_AT[b])) is not None:
                            q, s = t
                            last = NG // 2 - 1 if b == 0 else NG - 1
                            dve.wait_ge(s_av, gkey(q, NG * s + last, 1))
                            a = av[b][:, 0:(h1 - h0) * V1].rearrange("p (h d) -> p h d", d=V1)
                            nc.vector.reciprocal(rden[:, s, h0:h1].unsqueeze(2), a[:, :, HD:V1]).then_inc(s_rden, 1)
                            dve.wait_ge(s_rden, nkey(q, s) * 2 + (b + 1))
                            wait(dve, s_ot, nkey(q, s, -1))
                            nc.vector.tensor_tensor(
                                o32[:, s, HD * h0:HD * h1].rearrange("p (h d) -> p h d", d=HD), a[:, :, 0:HD],
                                rden[:, s, h0:h1].unsqueeze(2).to_broadcast([P, h1 - h0, HD]), ALU.mult).then_inc(s_o, 1)
                    if (t := tile_behind(p, j, OL_AT)) is not None:
                        q, s = t
                        dve.wait_ge(s_ohi, nkey(q, s, 1))
                        wait(dve, s_h, nkey(q, s, -1))
                        nc.vector.tensor_tensor(o_lo[:, s], tl[s][:].rearrange("p (c i) -> p c i", c=KC), o_hi[:, s],
                                                ALU.subtract).then_inc(s_olo, 1)
                    if (t := tile_behind(p, j, N_AT)) is not None:
                        q, s = t
                        dve.wait_ge(s_h, nkey(q, s, 1))
                        dve.wait_ge(s_prow[s], q * 16 + 16)
                        if known(q) and q == 0:
                            dve.wait_ge(s_down, 2)
                        wait(dve, s_h2b, nkey(q, s, -1))
                        nc.vector.scalar_tensor_tensor(out=h2[:, s, :], in0=tl[s][:], scalar=down[:, 1:2],
                                                       in1=prow[:, s, :], op0=ALU.mult, op1=ALU.add).then_inc(s_h2, 1)
                    if (t := tile_behind(p, j, ST_AT)) is not None:
                        q, s = t
                        dve.wait_ge(s_h2, nkey(q, s, 1))
                        nc.vector.bn_stats(st[:, s, :], h2[:, s, :]).then_inc(s_st, 1)
                        dve.wait_ge(s_down, 1)
                        dve.wait_ge(s_st, nkey(q, s, 1))
                        nc.vector.bn_aggr(mv[:, s, :], st[:, s, :]).then_inc(s_mv, 1)
                        dve.wait_ge(s_mv, nkey(q, s, 1))
                        wait(dve, s_rstd, nkey(q, s, -1))
                        nc.vector.tensor_scalar(vs[:, s:s + 1], mv[:, s, 1:2], LN_EPS, X_SCALE ** -2, ALU.add,
                                                ALU.mult).then_inc(s_vs, 1)
                    if (t := tile_behind(p, j, XN_AT)) is not None:
                        q, s = t
                        dve.wait_ge(s_rstd, nkey(q, s, 1))
                        wait(dve, s_xt, nkey(q, s, -1))
                        nc.vector.tensor_scalar(xn[:, s, :], h2[:, s, :], mv[:, s, 0:1], rstd[:, s:s + 1],
                                                ALU.subtract, ALU.mult).then_inc(s_xn, 1)
                    if (t := tile_behind(p, j, XL_AT)) is not None:
                        q, s = t
                        dve.wait_ge(s_xhi, nkey(q, s, 1))
                        wait(dve, s_y, nkey(q, s, -1))
                        nc.vector.tensor_tensor(x_lo[:, s], tl[s][:].rearrange("p (c i) -> p c i", c=KC), x_hi[:, s],
                                                ALU.subtract).then_inc(s_xlo, 1)
                    if (t := tile_behind(p, j, OUT_AT)) is not None:
                        q, s = t
                        dve.wait_ge(s_y, nkey(q, s, 1))
                        dve.wait_ge(s_h2b, nkey(q, s, 1))
                        wait(dve, s_store[s], q * 16)
                        nc.vector.scalar_tensor_tensor(out=y[:, s, :], in0=tl[s][:], scalar=thr[:, 3:4],
                                                       in1=h2b[:, s, :], op0=ALU.mult, op1=ALU.add).then_inc(s_out, 1)

            for p in range(PEELED):
                body(p)
            dve.reg_mov(scores_out, PEELED * SLOTS)
            with dve.Fori(PEELED, PAIRS - 1) as p:
                body(p)
            body(PAIRS - 1)
            body(PAIRS)
            body(PAIRS + 1)

        @block.tensor
        def _(pe):
            pe.wait_ge(s_const, 10)
            pe.wait_ge(s_lnt, 2)
            for half in range(2):
                for c in range(2):
                    cc = 2 * half + c
                    nc.tensor.transpose(tl[half][:, c * T:c * T + P], lnt[:, 0, cc * P:cc * P + P], ident[:])
                    mm = nc.tensor.transpose(tl[half][:, c * T + P:c * T + T], lnt[0:TB, 1, cc * P:cc * P + P],
                                             ident[0:TB, 0:TB])
                mm.then_inc(s_lntt_ps, 1)
            done_counts = iter(range(2 * TPB))

            def counts(n):
                for _ in range(n):
                    e = next(done_counts)
                    b2, c = divmod(e, TPB)
                    if e == 0:
                        pe.wait_ge(s_ohcol, B)
                    if c:
                        pe.wait_ge(s_ohsum, c)
                    if e == 0:
                        pe.wait_ge(s_lntt, 2)
                    wait(pe, s_cnt, 2 * (e - 1))
                    bank = tl[e % 2][:, 0:2 * T].rearrange("p (b t) -> p b t", b=2)
                    mm = nc.tensor.matmul(bank, tri[:], oh_col[:, 2 * b2:2 * b2 + 2, c, :], start=True, stop=(c == 0))
                    if c:
                        mm = nc.tensor.matmul(bank, ones16[:], oh_sum[:, 2 * b2:2 * b2 + 2, c, :],
                                              start=False, stop=True)
                    mm.then_inc(s_cnt_ps, 1)

            pe.wait_ge(s_lntt, 2)
            pe.wait_ge(s_wk, 16)
            for g in range(KC):
                for c in range(KC):
                    mm = nc.tensor.matmul(av[g // 2][:, (g % 2) * T:(g % 2) * T + T], wk[:, c, g * P:g * P + P],
                                          lnt_t[:, c, :], start=(c == 0), stop=(c == KC - 1), skip_group_check=True)
                if g % 2:
                    mm.then_inc(s_k_ps, 1)
            def by_id(w, banks, made, kc, counts_between):
                t0, n = ((0, P), (P, TB))[kc]
                for c in range(KC):
                    mm = nc.tensor.matmul(banks[kc][0:n, :], lnt_t[:, c, t0:t0 + n], w[:, c, :],
                                          start=(c == 0), stop=(c == KC - 1))
                    if c == KC - 1:
                        mm.then_inc(made, 1)
                    counts(counts_between[c])

            pe.wait_ge(s_wq, 16)
            by_id(wq, sc, s_q_ps, 0, (1, 1, 1, 1))
            by_id(wq, sc, s_q_ps, 1, (1, 1, 1, 1))
            pe.wait_ge(s_wv, 16)
            pe.wait_ge(s_ring_zero, 1)
            by_id(wv, ring, s_v_ps, 0, (1, 1, 0, 0))

            def gather(pair, u, bank, step):
                v, kc = divmod(step, 2)
                mm = nc.tensor.matmul(bank[:, v * 2 * P:(v + 1) * 2 * P],
                                      qstack[:, kc, UH * u + 2 * v:UH * u + 2 * v + 2, :, :].rearrange("p h r d -> p (h r d)"),
                                      oh_row[:, kc, bass.ds(pair * (2 * P), 2 * P)], start=(kc == 0), stop=(kc == 1))
                if step == 3:
                    mm.then_inc(s_ring_in, 1)

            pe.wait_ge(s_ohrow, 2)
            pe.wait_ge(s_qlo, 2)
            pe.wait_ge(s_qhi, 2)
            pe.wait_ge(s_zero, 3)
            for u in range(GU):
                wait(pe, s_ring_out, u - 1)
                for step in range(4):
                    gather(0, u, sc[u % 2], step)
            by_id(wv, ring, s_v_ps, 1, (1, 1, 1, 1))
            counts(2)
            pe.wait_ge(s_ring_out, GU)
            pe.wait_ge(s_ks, 2)
            pe.wait_ge(s_kst, 16 * (16 - len(KLO_BY_POOL)))
            pe.wait_ge(s_kst_pool, 16 * len(KLO_BY_POOL))

            def scores(p, j):
                s, g = j // NG, j % NG
                n = len(heads[g])
                for u in sorted({heads[g][0] // UH, heads[g][-1] // UH}):
                    pe.wait_ge(s_q4[u], p * 64 + 64)
                wait(pe, s_e, gkey(p, j, -1))
                for a, h in enumerate(heads[g]):
                    mm = nc.tensor.matmul(sc[j % 2][:, a * T:a * T + T], q4[:, h, s * P:s * P + P], kstack[:, h, :],
                                          start=True, stop=True, skip_group_check=True)
                mm.then_inc(s_score, 1)

            def transposes(p, j):
                q, jj = group_behind(p, j, LT)
                n = len(heads[jj % NG])
                e = ring_index(p, "t", j)
                pe.wait_ge(s_ring_out, e - 1)
                if known(p) and gkey(q, jj) == 0:
                    pe.wait_ge(s_va, 2)
                pe.wait_ge(s_weighted, gkey(q, jj, 1) * 2)
                bank, w = bank_at(p, "t", j), WC[:, jj % NW, :]
                for a in range(n):
                    nc.tensor.transpose(bank[:, a * P:a * P + P], w[:, a * P:a * P + P], ident[:])
                nc.tensor.transpose(bank[0:n * TB, n * P:n * P + P], w[:, n * P:n * T], ident[:]).then_inc(s_ring_in, 1)

            def attend(q, jj, step):
                s, g = jj // NG, jj % NG
                n = len(heads[g])
                b = 0 if heads[g][0] < HB0 else 1
                if step == 0:
                    pe.wait_ge(s_ring_out, ring_of_group(q, jj) + 1)
                    if known(q) and gkey(q, jj) == 0:
                        pe.wait_ge(s_va, 2)
                        pe.wait_ge(s_vrest, 16 * HG)
                    if heads[g][0] in (0, HB0):
                        wait(pe, s_o, nkey(q, s) * 2 + (b - 1))
                if step < n:
                    h = heads[g][step]
                    at = V1 * (h - HB0 * b)
                    nc.tensor.matmul(av[b][:, at:at + V1], WT[:, jj % NWT, step, :], v_a[:, h, :],
                                     start=(h in (0, HB0)), stop=False, skip_group_check=True)
                elif step == HG:
                    at = V1 * (heads[g][0] - HB0 * b)
                    nc.tensor.matmul(av[b][:, at:at + n * V1], WT[0:n * TB, jj % NWT, n, :], v_rest[0:n * TB, g, 0:n * V1],
                                     start=False, stop=(g in (NG // 2 - 1, NG - 1)), skip_group_check=True).then_inc(s_av, 1)

            def turn(src, s):
                for c in range(KC):
                    mm = nc.tensor.transpose(tl[s][:, c * P:c * P + P], src[:, s, c * P:c * P + P], ident[:])
                return mm

            wp_passes = [(c, a, b) for c in range(KC) for a, b in ((o_hi, wp_hi), (o_hi, wp_lo), (o_lo, wp_hi))]
            wf_passes = [(c, a, wtern) for a in (x_hi, x_lo) for c in range(KC)]

            def project(q, s, passes, which, step, ready, done, made_once):
                for k, i in enumerate(which):
                    if i is not None and k * STEPS // len(which) == step:
                        if i == 0:
                            pe.wait_ge(ready, nkey(q, s, 1))
                            if known(q) and q == 0:
                                pe.wait_ge(made_once, 1)
                        c, a, b = passes[i]
                        mm = nc.tensor.matmul(tl[s][:], a[:, s, c, :], b[:, c, :], start=(i == 0), stop=(i == len(passes) - 1))
                        if i == len(passes) - 1:
                            mm.then_inc(done, 1)

            STEPS = HG + 1

            def body(p):
                for j in range(SLOTS):
                    if group_behind(p, j, 0) is not None:
                        scores(p, j)
                    if group_behind(p, j, LT) is not None:
                        transposes(p, j)
                    for step in range(STEPS):
                        if (t := group_behind(p, j, LA)) is not None:
                            attend(*t, step)
                        if not known(p) or p < PAIRS - 1:
                            for u in units_after(j):
                                if step == 0:
                                    pe.wait_ge(s_ring_out, ring_index(p, "g", u) - 1)
                                gather(p + 1, u, bank_at(p, "g", u), step)
                        for at, which in H_AT.items():
                            if (t := tile_behind(p, j, at)) is not None:
                                project(*t, wp_passes, which, step, s_olo, s_h, s_wplo)
                        for at, which in Y_AT.items():
                            if (t := tile_behind(p, j, at)) is not None:
                                project(*t, wf_passes, which, step, s_xlo, s_y, s_wtern)
                    if (t := tile_behind(p, j, OT_AT)) is not None:
                        q, s = t
                        pe.wait_ge(s_o, nkey(q, s) * 2 + 2)
                        wait(pe, s_out, nkey(q, s, -1))
                        turn(o32, s).then_inc(s_ot, 1)
                    if (t := tile_behind(p, j, XT_AT)) is not None:
                        q, s = t
                        pe.wait_ge(s_xn, nkey(q, s, 1))
                        turn(xn, s).then_inc(s_xt, 1)

            for p in range(PEELED):
                body(p)
            with pe.Fori(PEELED, PAIRS - 1) as p:
                body(p)
            body(PAIRS - 1)
            body(PAIRS)
            body(PAIRS + 1)


def kernel(x, L0_tok_catid_time_matrix, L0_attn_Wq, L0_attn_Wk, L0_attn_Wv, L0_attn_Wp, L0_ffn_weight, L0_ffn_bias):
    import numpy as np
    import concourse.bacc as bacc
    from concourse.bass_utils import run_bass_kernel_spmd

    nc = bacc.Bacc("TRN2", target_bir_lowering=False, num_devices=1)
    arrays = {
        "ids": np.ascontiguousarray(x),
        "table": np.ascontiguousarray(L0_tok_catid_time_matrix),
        "wq_t": np.ascontiguousarray(np.asarray(L0_attn_Wq).T),
        "wk_t": np.ascontiguousarray(np.asarray(L0_attn_Wk).T),
        "wv_t": np.ascontiguousarray(np.asarray(L0_attn_Wv).T),
        "wp_t": np.ascontiguousarray(np.asarray(L0_attn_Wp).T),
        "wf_t": np.ascontiguousarray(np.asarray(L0_ffn_weight).T),
        "bias": np.ascontiguousarray(L0_ffn_bias),
    }
    args = [nc.dram_tensor(n, a.shape, mybir.dt.from_np(a.dtype), kind="ExternalInput").ap() for n, a in arrays.items()]
    shape = (*arrays["ids"].shape, arrays["table"].shape[1])
    out = nc.dram_tensor("out", shape, F32, kind="ExternalOutput").ap()
    scratch = nc.dram_tensor("probs_by_id", arrays["table"].shape, F32, kind="Internal").ap()
    lm_tower_kernel(nc, *args, out, scratch)
    result = run_bass_kernel_spmd(nc, [arrays], core_ids=[0])
    return result.results[0]["out"]
```
